# Optimizing a Trainium2 kernel written in Bass

```python
import numpy as np
import jax
import jax.numpy as jnp

def _softmax(x, axis=-1):
    return jax.nn.softmax(x, axis=axis)

def _gelu(x):
    return jax.nn.gelu(x, approximate=True)

def _silu(x):
    return jax.nn.silu(x)

def _sigmoid(x):
    return jax.nn.sigmoid(x)

def _layernorm(x, axis=-1, eps=1e-05):
    m = jnp.mean(x, axis=axis, keepdims=True)
    v = jnp.var(x, axis=axis, keepdims=True)
    return (x - m) / jnp.sqrt(v + eps)

def _scatter_add(tgt, idx, src, axis=0):
    return tgt.at[idx].add(src)

def _segment_sum(src, seg, n):
    return jax.ops.segment_sum(src, seg, n)
kernel_name = 'mk_adaln_d2_jaxref_r8_879c62'

def setup_inputs(seed: int=0):
    np.random.seed(seed)
    _w = jnp.asarray

    def _L0_attn_setup():
        import jax, jax.numpy as jnp
        import numpy as np
        DIM = 128
        STATE = 64
        HEADS = 8
        EXPAND = 2
        INNER = DIM * EXPAND
        HEAD_DIM = INNER // HEADS
        KERNEL = 4
        B, L = (2, 256)
        EPS = 1e-05

        def _causal_conv(x, conv_w, conv_b):
            x_pad = jnp.pad(x, ((0, 0), (KERNEL - 1, 0), (0, 0)))
            w = conv_w[:, 0, :]
            y = sum((x_pad[:, k:k + x.shape[1], :] * w[:, k] for k in range(KERNEL)))
            return y + conv_b

        def _ssd_scan(x, b, c, dt, a):
            state0 = jnp.zeros((x.shape[0], HEADS, STATE, HEAD_DIM), x.dtype)

            def step(state, inp):
                x_t, b_t, c_t, dt_t = inp
                decay = jnp.exp(dt_t * a)[..., None, None]
                b_bar = dt_t[..., None] * b_t
                state = decay * state + b_bar[..., None] * x_t[:, :, None, :]
                y_t = jnp.einsum('bhn,bhnp->bhp', c_t, state)
                return (state, y_t)
            xs = (x.transpose(1, 0, 2, 3), b.transpose(1, 0, 2, 3), c.transpose(1, 0, 2, 3), dt.transpose(1, 0, 2))
            _, ys = jax.lax.scan(step, state0, xs)
            return ys.transpose(1, 0, 2, 3)
        key = jax.random.key(seed)
        ks = jax.random.split(key, 12)
        s = 0.02
        return {'input_tensor': jax.random.normal(ks[0], (B, L, DIM), jnp.float32), 'Wx': jax.random.normal(ks[1], (INNER, DIM), jnp.float32) * s, 'Wz': jax.random.normal(ks[2], (INNER, DIM), jnp.float32) * s, 'conv_w': jax.random.normal(ks[3], (INNER, 1, KERNEL), jnp.float32) * s, 'conv_b': jnp.zeros((INNER,), jnp.float32), 'Wb': jax.random.normal(ks[4], (HEADS * STATE, INNER), jnp.float32) * s, 'Wc': jax.random.normal(ks[5], (HEADS * STATE, INNER), jnp.float32) * s, 'Wdt': jax.random.normal(ks[6], (HEADS, INNER), jnp.float32) * s, 'b_dt': jnp.zeros((HEADS,), jnp.float32), 'log_a': jnp.log(jnp.full((HEADS,), 0.5, jnp.float32)), 'd_param': jnp.ones((HEADS,), jnp.float32), 'gn_w': jnp.ones((INNER,), jnp.float32), 'gn_b': jnp.zeros((INNER,), jnp.float32), 'Wout': jax.random.normal(ks[7], (DIM, INNER), jnp.float32) * s}
    _L0_attn_in = _L0_attn_setup()

    def _L0_ffn_setup():
        import jax, jax.numpy as jnp
        import numpy as np
        DIM = 128
        DEPTH = 6
        HEADS = 16
        DIM_HEAD = 64
        WINDOW = 32
        INNER = HEADS * DIM_HEAD
        DIM_INNER = int(DIM * 4 * 2 / 3)
        QK_SCALE = 8.0

        def shift_tokens(t):
            a, s = jnp.split(t, 2, -1)
            s = jnp.pad(s, ((0, 0), (1, 0), (0, 0)))[:, :-1]
            return jnp.concatenate([a, s], -1)

        def l2norm(t):
            return t / jnp.maximum(jnp.linalg.norm(t, axis=-1, keepdims=True), 1e-12)

        def rotate_half(x):
            x1, x2 = jnp.split(x, 2, -1)
            return jnp.concatenate([-x2, x1], -1)

        def rotary_tables(n):
            half = jnp.arange(0, DIM_HEAD, 2, dtype=jnp.float32)
            inv_freq = 1.0 / 10000.0 ** (half / DIM_HEAD)
            t = jnp.arange(n, dtype=jnp.float32)
            freqs = t[:, None] * inv_freq[None, :]
            freqs = jnp.concatenate([freqs, freqs], -1)
            base_scale = (half + 0.4 * DIM_HEAD) / (1.4 * DIM_HEAD)
            power = (t - n // 2) / (WINDOW // 2)
            scale = base_scale[None, :] ** power[:, None]
            scale = jnp.concatenate([scale, scale], -1)
            return (freqs, scale)

        def local_attention(q, k, v):
            b, h, n, d = q.shape
            w = WINDOW
            nw = n // w
            bq = q.reshape(b, h, nw, w, d)
            bk = k.reshape(b, h, nw, w, d)
            bv = v.reshape(b, h, nw, w, d)

            def look(t):
                p = jnp.pad(t, ((0, 0), (0, 0), (1, 0), (0, 0), (0, 0)))
                return jnp.concatenate([p[:, :, :nw], p[:, :, 1:]], axis=3)
            bk2, bv2 = (look(bk), look(bv))
            seq = jnp.arange(n).reshape(nw, w)
            seq_p = jnp.pad(seq, ((1, 0), (0, 0)), constant_values=-1)
            jt = jnp.concatenate([seq_p[:nw], seq_p[1:]], axis=1)
            it = seq[:, :, None]
            jb = jt[:, None, :]
            mask = (it < jb) | (it > jb + w) | (jb == -1)
            sim = jnp.einsum('bhwie,bhwje->bhwij', bq, bk2) * QK_SCALE
            sim = jnp.where(mask, -jnp.finfo(sim.dtype).max, sim)
            attn = jax.nn.softmax(sim, -1)
            out = jnp.einsum('bhwij,bhwje->bhwie', attn, bv2)
            return out.reshape(b, h, n, d)

        def attn_layer(x, Wqkv, qs, ksc, Wo):
            b, n, _ = x.shape
            qkv = x @ Wqkv
            q, k, v = jnp.split(qkv, 3, -1)
            sh = lambda t: t.reshape(b, n, HEADS, DIM_HEAD).transpose(0, 2, 1, 3)
            q, k, v = (sh(q), sh(k), sh(v))
            q = l2norm(q) * qs
            k = l2norm(k) * ksc
            freqs, scale = rotary_tables(n)
            cos, sin = (jnp.cos(freqs), jnp.sin(freqs))
            q = q * cos * scale + rotate_half(q) * sin * scale
            inv = 1.0 / scale
            k = k * cos * inv + rotate_half(k) * sin * inv
            out = local_attention(q, k, v)
            out = out.transpose(0, 2, 1, 3).reshape(b, n, INNER)
            return out @ Wo

        def ffn_layer(x, g, bln, W1, b1, W2, b2):
            mu = x.mean(-1, keepdims=True)
            var = ((x - mu) ** 2).mean(-1, keepdims=True)
            xn = (x - mu) / jnp.sqrt(var + 1e-05) * g + bln
            hg = xn @ W1 + b1
            a, gate = jnp.split(hg, 2, -1)
            return a * jax.nn.gelu(gate, approximate=False) @ W2 + b2
        key = jax.random.key(seed)
        ks = jax.random.split(key, 8)
        B, N = (2, 256)
        init = lambda k, shape: jax.random.normal(k, shape, jnp.float32) * 0.02
        return {'x': jax.random.normal(ks[0], (B, N, DIM), jnp.float32), 'Wqkv': init(ks[1], (DEPTH, DIM, 3 * INNER)), 'q_scale': jnp.ones((DEPTH, DIM_HEAD), jnp.float32), 'k_scale': jnp.ones((DEPTH, DIM_HEAD), jnp.float32), 'Wo': init(ks[2], (DEPTH, INNER, DIM)), 'ln_g': jnp.ones((DEPTH, DIM), jnp.float32), 'ln_b': jnp.zeros((DEPTH, DIM), jnp.float32), 'W1': init(ks[3], (DEPTH, DIM, 2 * DIM_INNER)), 'b1': jnp.zeros((DEPTH, 2 * DIM_INNER), jnp.float32), 'W2': init(ks[4], (DEPTH, DIM_INNER, DIM)), 'b2': jnp.zeros((DEPTH, DIM), jnp.float32)}
    _L0_ffn_in = _L0_ffn_setup()
    _L0_c = _w((lambda *s: np.random.randn(*s).astype(np.float32) * 0.05)(4, 128))
    _L0_wmod = _w((lambda *s: np.random.randn(*s).astype(np.float32) * 0.05)(128, 6 * 128) * 128 ** (-0.5))

    def _L1_attn_setup():
        import jax, jax.numpy as jnp
        import numpy as np
        B, T = (4, 256)
        D_MODEL = 128
        N_HEADS = 8
        HEAD_DIM = 32
        KV_LRANK = 64

        def _orthogonalize_per_head(w):
            chunks = w.reshape(N_HEADS, HEAD_DIM, D_MODEL)

            def ns(m):
                A = m @ m.T
                Bm = 1.5 * jnp.eye(HEAD_DIM, dtype=m.dtype) - 0.5 * A
                return Bm @ m
            return jax.vmap(ns)(chunks).reshape(w.shape)
        key = jax.random.key(seed)
        ks = jax.random.split(key, 6)

        def lin(k, out_dim, in_dim):
            bound = 1.0 / np.sqrt(in_dim)
            return jax.random.uniform(k, (out_dim, in_dim), jnp.float32, -bound, bound)
        Wq = _orthogonalize_per_head(lin(ks[0], N_HEADS * HEAD_DIM, D_MODEL))
        return {'x': jax.random.normal(ks[1], (B, T, D_MODEL), jnp.float32), 'Wq': Wq, 'Wkv_down': lin(ks[2], KV_LRANK, D_MODEL), 'Wk_up': lin(ks[3], N_HEADS * HEAD_DIM, KV_LRANK), 'Wv_up': lin(ks[4], N_HEADS * HEAD_DIM, KV_LRANK), 'Wo': lin(ks[5], D_MODEL, N_HEADS * HEAD_DIM)}
    _L1_attn_in = _L1_attn_setup()

    def _L1_ffn_setup():
        import jax, jax.numpy as jnp
        import numpy as np
        D_MODEL = 128
        H_SHARED = 256
        H_ROUTED = 128
        N_EXPERTS = 8
        TOP_K = 2
        key = jax.random.key(seed)
        ks = jax.random.split(key, 8)
        B, T = (2, 256)
        sc_d = 1.0 / np.sqrt(D_MODEL)
        sc_hs = 1.0 / np.sqrt(H_SHARED)
        sc_hr = 1.0 / np.sqrt(H_ROUTED)
        return {'x': jax.random.normal(ks[0], (B, T, D_MODEL), dtype=jnp.float32), 'router_w': jax.random.normal(ks[1], (N_EXPERTS, D_MODEL), dtype=jnp.float32) * sc_d, 'router_bias': jnp.zeros((N_EXPERTS,), dtype=jnp.float32), 'sw1': jax.random.normal(ks[2], (D_MODEL, H_SHARED), dtype=jnp.float32) * sc_d, 'sw3': jax.random.normal(ks[3], (D_MODEL, H_SHARED), dtype=jnp.float32) * sc_d, 'sw2': jax.random.normal(ks[4], (H_SHARED, D_MODEL), dtype=jnp.float32) * sc_hs, 'ew1': jax.random.normal(ks[5], (N_EXPERTS, D_MODEL, H_ROUTED), dtype=jnp.float32) * sc_d, 'ew2': jax.random.normal(ks[6], (N_EXPERTS, H_ROUTED, D_MODEL), dtype=jnp.float32) * sc_hr}
    _L1_ffn_in = _L1_ffn_setup()
    _L1_c = _w((lambda *s: np.random.randn(*s).astype(np.float32) * 0.05)(4, 128))
    _L1_wmod = _w((lambda *s: np.random.randn(*s).astype(np.float32) * 0.05)(128, 6 * 128) * 128 ** (-0.5))
    _d = {'L0_attn_input_tensor': _L0_attn_in['input_tensor'], 'L0_attn_Wx': _L0_attn_in['Wx'], 'L0_attn_Wz': _L0_attn_in['Wz'], 'L0_attn_conv_w': _L0_attn_in['conv_w'], 'L0_attn_conv_b': _L0_attn_in['conv_b'], 'L0_attn_Wb': _L0_attn_in['Wb'], 'L0_attn_Wc': _L0_attn_in['Wc'], 'L0_attn_Wdt': _L0_attn_in['Wdt'], 'L0_attn_b_dt': _L0_attn_in['b_dt'], 'L0_attn_log_a': _L0_attn_in['log_a'], 'L0_attn_d_param': _L0_attn_in['d_param'], 'L0_attn_gn_w': _L0_attn_in['gn_w'], 'L0_attn_gn_b': _L0_attn_in['gn_b'], 'L0_attn_Wout': _L0_attn_in['Wout'], 'L0_ffn_Wqkv': _L0_ffn_in['Wqkv'], 'L0_ffn_q_scale': _L0_ffn_in['q_scale'], 'L0_ffn_k_scale': _L0_ffn_in['k_scale'], 'L0_ffn_Wo': _L0_ffn_in['Wo'], 'L0_ffn_ln_g': _L0_ffn_in['ln_g'], 'L0_ffn_ln_b': _L0_ffn_in['ln_b'], 'L0_ffn_W1': _L0_ffn_in['W1'], 'L0_ffn_b1': _L0_ffn_in['b1'], 'L0_ffn_W2': _L0_ffn_in['W2'], 'L0_ffn_b2': _L0_ffn_in['b2'], 'L0_c': _L0_c, 'L0_wmod': _L0_wmod, 'L1_attn_Wq': _L1_attn_in['Wq'], 'L1_attn_Wkv_down': _L1_attn_in['Wkv_down'], 'L1_attn_Wk_up': _L1_attn_in['Wk_up'], 'L1_attn_Wv_up': _L1_attn_in['Wv_up'], 'L1_attn_Wo': _L1_attn_in['Wo'], 'L1_ffn_router_w': _L1_ffn_in['router_w'], 'L1_ffn_router_bias': _L1_ffn_in['router_bias'], 'L1_ffn_sw1': _L1_ffn_in['sw1'], 'L1_ffn_sw3': _L1_ffn_in['sw3'], 'L1_ffn_sw2': _L1_ffn_in['sw2'], 'L1_ffn_ew1': _L1_ffn_in['ew1'], 'L1_ffn_ew2': _L1_ffn_in['ew2'], 'L1_c': _L1_c, 'L1_wmod': _L1_wmod}
    _x0 = _d['L0_attn_input_tensor']
    _d['L0_attn_input_tensor'] = jax.random.normal(jax.random.fold_in(jax.random.key(seed), 1), (4, 512, 128), dtype=_x0.dtype)
    del _x0
    return _d

def reference(L0_attn_input_tensor, L0_attn_Wx, L0_attn_Wz, L0_attn_conv_w, L0_attn_conv_b, L0_attn_Wb, L0_attn_Wc, L0_attn_Wdt, L0_attn_b_dt, L0_attn_log_a, L0_attn_d_param, L0_attn_gn_w, L0_attn_gn_b, L0_attn_Wout, L0_ffn_Wqkv, L0_ffn_q_scale, L0_ffn_k_scale, L0_ffn_Wo, L0_ffn_ln_g, L0_ffn_ln_b, L0_ffn_W1, L0_ffn_b1, L0_ffn_W2, L0_ffn_b2, L0_c, L0_wmod, L1_attn_Wq, L1_attn_Wkv_down, L1_attn_Wk_up, L1_attn_Wv_up, L1_attn_Wo, L1_ffn_router_w, L1_ffn_router_bias, L1_ffn_sw1, L1_ffn_sw3, L1_ffn_sw2, L1_ffn_ew1, L1_ffn_ew2, L1_c, L1_wmod):

    def _L0_attn_ref(input_tensor, Wx, Wz, conv_w, conv_b, Wb, Wc, Wdt, b_dt, log_a, d_param, gn_w, gn_b, Wout):
        import jax, jax.numpy as jnp
        import numpy as np
        DIM = 128
        STATE = 64
        HEADS = 8
        EXPAND = 2
        INNER = DIM * EXPAND
        HEAD_DIM = INNER // HEADS
        KERNEL = 4
        B, L = (2, 256)
        EPS = 1e-05

        def _causal_conv(x, conv_w, conv_b):
            x_pad = jnp.pad(x, ((0, 0), (KERNEL - 1, 0), (0, 0)))
            w = conv_w[:, 0, :]
            y = sum((x_pad[:, k:k + x.shape[1], :] * w[:, k] for k in range(KERNEL)))
            return y + conv_b

        def _ssd_scan(x, b, c, dt, a):
            state0 = jnp.zeros((x.shape[0], HEADS, STATE, HEAD_DIM), x.dtype)

            def step(state, inp):
                x_t, b_t, c_t, dt_t = inp
                decay = jnp.exp(dt_t * a)[..., None, None]
                b_bar = dt_t[..., None] * b_t
                state = decay * state + b_bar[..., None] * x_t[:, :, None, :]
                y_t = jnp.einsum('bhn,bhnp->bhp', c_t, state)
                return (state, y_t)
            xs = (x.transpose(1, 0, 2, 3), b.transpose(1, 0, 2, 3), c.transpose(1, 0, 2, 3), dt.transpose(1, 0, 2))
            _, ys = jax.lax.scan(step, state0, xs)
            return ys.transpose(1, 0, 2, 3)
        bsz, seq, _ = input_tensor.shape
        x = input_tensor @ Wx.T
        z = input_tensor @ Wz.T
        x = _causal_conv(x, conv_w, conv_b)
        x = jax.nn.silu(x)
        b = (x @ Wb.T).reshape(bsz, seq, HEADS, STATE)
        c = (x @ Wc.T).reshape(bsz, seq, HEADS, STATE)
        dt = jax.nn.softplus(x @ Wdt.T + b_dt)
        xh = x.reshape(bsz, seq, HEADS, HEAD_DIM)
        a = -jnp.exp(log_a)
        y = _ssd_scan(xh, b, c, dt, a)
        y = y + d_param[None, None, :, None] * xh
        yg = y
        mean = yg.mean(axis=(1, 3), keepdims=True)
        var = yg.var(axis=(1, 3), keepdims=True)
        yn = (yg - mean) / jnp.sqrt(var + EPS)
        yn = yn * gn_w.reshape(1, 1, HEADS, HEAD_DIM) + gn_b.reshape(1, 1, HEADS, HEAD_DIM)
        yn = yn.reshape(bsz, seq, INNER)
        out = yn * jax.nn.silu(z)
        return out @ Wout.T

    def _L0_ffn_ref(x, Wqkv, q_scale, k_scale, Wo, ln_g, ln_b, W1, b1, W2, b2):
        import jax, jax.numpy as jnp
        import numpy as np
        DIM = 128
        DEPTH = 6
        HEADS = 16
        DIM_HEAD = 64
        WINDOW = 32
        INNER = HEADS * DIM_HEAD
        DIM_INNER = int(DIM * 4 * 2 / 3)
        QK_SCALE = 8.0

        def shift_tokens(t):
            a, s = jnp.split(t, 2, -1)
            s = jnp.pad(s, ((0, 0), (1, 0), (0, 0)))[:, :-1]
            return jnp.concatenate([a, s], -1)

        def l2norm(t):
            return t / jnp.maximum(jnp.linalg.norm(t, axis=-1, keepdims=True), 1e-12)

        def rotate_half(x):
            x1, x2 = jnp.split(x, 2, -1)
            return jnp.concatenate([-x2, x1], -1)

        def rotary_tables(n):
            half = jnp.arange(0, DIM_HEAD, 2, dtype=jnp.float32)
            inv_freq = 1.0 / 10000.0 ** (half / DIM_HEAD)
            t = jnp.arange(n, dtype=jnp.float32)
            freqs = t[:, None] * inv_freq[None, :]
            freqs = jnp.concatenate([freqs, freqs], -1)
            base_scale = (half + 0.4 * DIM_HEAD) / (1.4 * DIM_HEAD)
            power = (t - n // 2) / (WINDOW // 2)
            scale = base_scale[None, :] ** power[:, None]
            scale = jnp.concatenate([scale, scale], -1)
            return (freqs, scale)

        def local_attention(q, k, v):
            b, h, n, d = q.shape
            w = WINDOW
            nw = n // w
            bq = q.reshape(b, h, nw, w, d)
            bk = k.reshape(b, h, nw, w, d)
            bv = v.reshape(b, h, nw, w, d)

            def look(t):
                p = jnp.pad(t, ((0, 0), (0, 0), (1, 0), (0, 0), (0, 0)))
                return jnp.concatenate([p[:, :, :nw], p[:, :, 1:]], axis=3)
            bk2, bv2 = (look(bk), look(bv))
            seq = jnp.arange(n).reshape(nw, w)
            seq_p = jnp.pad(seq, ((1, 0), (0, 0)), constant_values=-1)
            jt = jnp.concatenate([seq_p[:nw], seq_p[1:]], axis=1)
            it = seq[:, :, None]
            jb = jt[:, None, :]
            mask = (it < jb) | (it > jb + w) | (jb == -1)
            sim = jnp.einsum('bhwie,bhwje->bhwij', bq, bk2) * QK_SCALE
            sim = jnp.where(mask, -jnp.finfo(sim.dtype).max, sim)
            attn = jax.nn.softmax(sim, -1)
            out = jnp.einsum('bhwij,bhwje->bhwie', attn, bv2)
            return out.reshape(b, h, n, d)

        def attn_layer(x, Wqkv, qs, ksc, Wo):
            b, n, _ = x.shape
            qkv = x @ Wqkv
            q, k, v = jnp.split(qkv, 3, -1)
            sh = lambda t: t.reshape(b, n, HEADS, DIM_HEAD).transpose(0, 2, 1, 3)
            q, k, v = (sh(q), sh(k), sh(v))
            q = l2norm(q) * qs
            k = l2norm(k) * ksc
            freqs, scale = rotary_tables(n)
            cos, sin = (jnp.cos(freqs), jnp.sin(freqs))
            q = q * cos * scale + rotate_half(q) * sin * scale
            inv = 1.0 / scale
            k = k * cos * inv + rotate_half(k) * sin * inv
            out = local_attention(q, k, v)
            out = out.transpose(0, 2, 1, 3).reshape(b, n, INNER)
            return out @ Wo

        def ffn_layer(x, g, bln, W1, b1, W2, b2):
            mu = x.mean(-1, keepdims=True)
            var = ((x - mu) ** 2).mean(-1, keepdims=True)
            xn = (x - mu) / jnp.sqrt(var + 1e-05) * g + bln
            hg = xn @ W1 + b1
            a, gate = jnp.split(hg, 2, -1)
            return a * jax.nn.gelu(gate, approximate=False) @ W2 + b2
        for i in range(DEPTH):
            x = attn_layer(shift_tokens(x), Wqkv[i], q_scale[i], k_scale[i], Wo[i]) + x
            x = ffn_layer(shift_tokens(x), ln_g[i], ln_b[i], W1[i], b1[i], W2[i], b2[i]) + x
        return x

    def _L1_attn_ref(x, Wq, Wkv_down, Wk_up, Wv_up, Wo):
        import jax, jax.numpy as jnp
        import numpy as np
        B, T = (4, 256)
        D_MODEL = 128
        N_HEADS = 8
        HEAD_DIM = 32
        KV_LRANK = 64

        def _orthogonalize_per_head(w):
            chunks = w.reshape(N_HEADS, HEAD_DIM, D_MODEL)

            def ns(m):
                A = m @ m.T
                Bm = 1.5 * jnp.eye(HEAD_DIM, dtype=m.dtype) - 0.5 * A
                return Bm @ m
            return jax.vmap(ns)(chunks).reshape(w.shape)
        b, t, _ = x.shape
        q = (x @ Wq.T).reshape(b, t, N_HEADS, HEAD_DIM)
        kv_latent = x @ Wkv_down.T
        k = (kv_latent @ Wk_up.T).reshape(b, t, N_HEADS, HEAD_DIM)
        v = (kv_latent @ Wv_up.T).reshape(b, t, N_HEADS, HEAD_DIM)
        scale = HEAD_DIM ** (-0.5)
        scores = jnp.einsum('bqhd,bkhd->bhqk', q, k) * scale
        attn = jax.nn.softmax(scores, axis=-1)
        out = jnp.einsum('bhqk,bkhd->bqhd', attn, v)
        out = out.reshape(b, t, N_HEADS * HEAD_DIM)
        return out @ Wo.T

    def _L1_ffn_ref(x, router_w, router_bias, sw1, sw3, sw2, ew1, ew2):
        import jax, jax.numpy as jnp
        import numpy as np
        D_MODEL = 128
        H_SHARED = 256
        H_ROUTED = 128
        N_EXPERTS = 8
        TOP_K = 2
        B, T, C = x.shape
        xf = x.reshape(-1, C)
        shared_out = jax.nn.silu(xf @ sw1) * (xf @ sw3) @ sw2
        s = jax.nn.sigmoid((xf @ router_w.T).astype(jnp.float32))
        sel_scores = s + router_bias.astype(jnp.float32)
        _, topk_idx = jax.lax.top_k(sel_scores, TOP_K)
        s_sel = jnp.take_along_axis(s, topk_idx, axis=1)
        denom = s_sel.sum(axis=1, keepdims=True)
        gates = jnp.where(denom > 1e-09, s_sel / (denom + 1e-09), 1.0 / TOP_K).astype(x.dtype)
        one_hot = jax.nn.one_hot(topk_idx, N_EXPERTS, dtype=x.dtype)
        comb = jnp.einsum('nke,nk->ne', one_hot, gates)
        h = jax.nn.gelu(jnp.einsum('nd,edh->neh', xf, ew1), approximate=False)
        y = jnp.einsum('neh,ehd->ned', h, ew2)
        routed_out = jnp.einsum('ned,ne->nd', y, comb)
        return (shared_out + routed_out).reshape(B, T, C)
    x = L0_attn_input_tensor
    mod = (_silu(L0_c) @ L0_wmod).reshape(L0_c.shape[0], 6, 1, -1)
    sa, ca, ga, sb, cb, gb = (mod[:, 0], mod[:, 1], mod[:, 2], mod[:, 3], mod[:, 4], mod[:, 5])
    ga = (2 * (ga >= 0) - 1) * jnp.maximum(jnp.abs(ga), 0.25)
    gb = (2 * (gb >= 0) - 1) * jnp.maximum(jnp.abs(gb), 0.25)
    h = _layernorm(x, axis=-1) * (1 + ca) + sa
    x = x + ga * _L0_attn_ref(h, L0_attn_Wx, L0_attn_Wz, L0_attn_conv_w, L0_attn_conv_b, L0_attn_Wb, L0_attn_Wc, L0_attn_Wdt, L0_attn_b_dt, L0_attn_log_a, L0_attn_d_param, L0_attn_gn_w, L0_attn_gn_b, L0_attn_Wout)
    h = _layernorm(x, axis=-1) * (1 + cb) + sb
    x = x + gb * _L0_ffn_ref(h, L0_ffn_Wqkv, L0_ffn_q_scale, L0_ffn_k_scale, L0_ffn_Wo, L0_ffn_ln_g, L0_ffn_ln_b, L0_ffn_W1, L0_ffn_b1, L0_ffn_W2, L0_ffn_b2)
    mod = (_silu(L1_c) @ L1_wmod).reshape(L1_c.shape[0], 6, 1, -1)
    sa, ca, ga, sb, cb, gb = (mod[:, 0], mod[:, 1], mod[:, 2], mod[:, 3], mod[:, 4], mod[:, 5])
    ga = (2 * (ga >= 0) - 1) * jnp.maximum(jnp.abs(ga), 0.25)
    gb = (2 * (gb >= 0) - 1) * jnp.maximum(jnp.abs(gb), 0.25)
    h = _layernorm(x, axis=-1) * (1 + ca) + sa
    x = x + ga * _L1_attn_ref(h, L1_attn_Wq, L1_attn_Wkv_down, L1_attn_Wk_up, L1_attn_Wv_up, L1_attn_Wo)
    h = _layernorm(x, axis=-1) * (1 + cb) + sb
    x = x + gb * _L1_ffn_ref(h, L1_ffn_router_w, L1_ffn_router_bias, L1_ffn_sw1, L1_ffn_sw3, L1_ffn_sw2, L1_ffn_ew1, L1_ffn_ew2)
    return x

_drawn_inputs = setup_inputs


def setup_inputs(seed=0):
    import zlib

    import numpy as np

    out = dict(_drawn_inputs(seed))
    spreads = {'L0_attn_conv_b': (0.0, 0.483),
     'L0_attn_b_dt': (0.0, 0.8),
     'L0_attn_log_a': (-0.6931471824645996, 0.6),
     'L0_attn_d_param': (1.0, 0.6),
     'L0_attn_gn_w': (1.0, 0.6),
     'L0_attn_gn_b': (0.0, 0.8),
     'L0_ffn_q_scale': (1.0, 0.6),
     'L0_ffn_k_scale': (1.0, 0.6),
     'L0_ffn_ln_g': (1.0, 0.6),
     'L0_ffn_ln_b': (0.0, 0.8),
     'L0_ffn_b1': (0.0, 0.8),
     'L0_ffn_b2': (0.0, 0.1),
     'L1_ffn_router_bias': (0.0, 0.8)}
    factors = {'L0_attn_Wx': 8.0,
     'L0_attn_Wz': 4.124,
     'L0_attn_conv_w': 8.0,
     'L0_attn_Wb': 8.0,
     'L0_attn_Wc': 8.0,
     'L0_attn_Wdt': 8.0,
     'L0_attn_Wout': 4.253,
     'L0_ffn_W1': 4.977,
     'L0_ffn_W2': 5.235,
     'L1_attn_Wq': 8.0,
     'L1_attn_Wkv_down': 8.0,
     'L1_attn_Wk_up': 8.0,
     'L1_attn_Wv_up': 7.787,
     'L1_attn_Wo': 7.428,
     'L1_ffn_router_w': 8.0,
     'L1_ffn_sw1': 8.0,
     'L1_ffn_sw3': 8.0,
     'L1_ffn_sw2': 8.0,
     'L1_ffn_ew1': 8.0,
     'L1_ffn_ew2': 8.0}
    for name, (base, spread) in spreads.items():
        noise = np.random.default_rng([zlib.crc32(name.encode()), seed]).standard_normal(out[name].shape)
        drawn = base * np.exp(spread * noise) if base else spread * noise
        out[name] = jnp.asarray(drawn.astype(out[name].dtype))
    for name, factor in factors.items():
        out[name] = (out[name] * factor).astype(out[name].dtype)
    return out
```

```python
from contextlib import ExitStack

import numpy as np
import concourse.bass as bass
from concourse import mybir

F32 = mybir.dt.float32
ALU = mybir.AluOpType
ACT = mybir.ActivationFunctionType
AX = mybir.AxisListType

B, L, D = 4, 512, 128
P = 128
NT = L // P
EPS = 1e-5
GATE_MIN = 0.25
SH, SN, SP = 8, 64, 32
INNER = SH * SP
FM = INNER // P
TAPS = 4
PAIRS = SH // 2
STEPS_A = PAIRS * NT
DEPTH, QH, QD, WIN = 6, 16, 64, 32
GH = 4
NG = QH // GH
GW = GH * QD
NW = P // WIN
UNITS = NG * B * NT
PASSES = NG * B
QK_SCALE = 8.0
NORM_MIN = 1e-12
PADX = WIN + 1
FF = 341
FR = [P, P, FF - 2 * P]
FK = len(FR)
MASKED = -1.0e30
AH, AD, AR = 8, 32, 64
NE = 8
SM_SCALE = AD ** -0.5
DENOM_MIN = 1e-9


class Steps:

    def __init__(self, eng, sem):
        self.eng, self.sem, self.base, self.n, self.held = eng, sem, 0, 0, []

    def did(self, ins):
        ins.then_inc(self.sem, 1)
        self.n += 1
        return self.n

    def wait(self, at=None):
        self.eng.wait_ge(self.sem, self.base + (self.n if at is None else at))

    def enter(self, i, per):
        self.held.append((self.base, self.n))
        self.base, self.n = self.base + self.n + i * per, 0

    def leave(self, trips, per):
        assert self.n == per, f"{self.n} steps in a pass, not {per}"
        self.base, self.n = self.held.pop()
        self.n += trips * per


def mixer(nc, t, XR, X, XA, mod, PS, onesm, ident, epsc, sel8):
    with ExitStack() as ctx:
        def sb(name, shape):
            return ctx.enter_context(nc.sbuf_tensor(name, shape, F32))

        def sem(name):
            return ctx.enter_context(nc.semaphore(name))

        grpm = sb("grpm", [P, P])
        tri = sb("tri", [P, P])
        cT = sb("cT", [P, 2, B])
        wmod = sb("wmod", [P, 2, 6 * D])
        wxz = sb("wxz", [P, 2, INNER])
        convp = sb("convp", [P, FM, TAPS + 1])
        wbc = sb("wbc", [P, 2, FM, SH * SN])
        wdt = sb("wdt", [P, FM, SH])
        head8 = sb("head8", [SH, 2])
        featp = sb("featp", [P, FM, 3])
        wout = sb("wout", [P, FM, D])
        sc = sb("sc", [P, 2, B])
        gtmp = sb("gtmp", [P, 4, 4, B])
        lnc = sb("lnc", [P, L])
        lnsq = sb("lnsq", [P, L])
        lnv = sb("lnv", [P, L])
        lnr = sb("lnr", [P, L])
        lnt = sb("lnt", [P, L])
        hT = sb("hT", [P, L])
        xpad = sb("xpad", [P, FM, TAPS - 1 + L])
        cacc = sb("cacc", [P, FM, TAPS, L])
        xc = sb("xc", [P, FM, L])
        zs = sb("zs", [P, FM, L])
        d8 = sb("d8", [SH, 8, L])
        neg_a = sb("neg_a", [SH, 2])
        cols = sb("cols", [P, 2, NT, SH])
        xdt = sb("xdt", [P, NT, INNER])
        bcT = sb("bcT", [P, 2, PAIRS, L])
        dec = sb("dec", [P, 2, 2, L])
        wgt = sb("wgt", [P, 2, 2, L])
        ysb = sb("ysb", [P, FM, L])
        bst = sb("bst", [P, FM, 6])
        gst = sb("gst", [P, 2, FM])
        gsm = sb("gsm", [P, 2, FM])
        gv = sb("gv", [P, 8, FM])
        mhalf = sb("mhalf", [P, FM])
        yn = sb("yn", [P, FM, L])
        onorm = sb("onorm", [P, FM, L])

        landed = sem("a_landed")
        weights = sem("a_weights")
        zeroed = sem("a_zeroed")
        silu_c = sem("silu_c")
        mod_mm = sem("mod_mm")
        mod_ready = sem("mod_ready")
        dve_steps = sem("a_dve_steps")
        act_steps = sem("a_act_steps")
        ln_in = sem("a_ln_in")
        ln_mean = sem("a_ln_mean")
        ln_cent = sem("a_ln_cent")
        ln_sq = sem("a_ln_sq")
        ln_var = sem("a_ln_var")
        ln_rstd = sem("a_ln_rstd")
        h_ready = sem("h_ready")
        a_done = sem("a_done")
        xz_mm = sem("xz_mm")
        xpad_ready = sem("xpad_ready")
        conv_ready = sem("conv_ready")
        xc_ready = sem("xc_ready")
        zs_ready = sem("zs_ready")
        dt_mm = sem("dt_mm")
        dt_na = sem("dt_na")
        dt_ln = sem("dt_ln")
        acum_ready = sem("acum_ready")
        col_tr = sem("col_tr")
        col_ready = sem("col_ready")
        xtok_tr = sem("xtok_tr")
        xdt_ready = sem("xdt_ready")
        bc_mm = sem("bc_mm")
        bc_ready = sem("bc_ready")
        ab_mm = sem("ab_mm")
        g_mm = sem("g_mm")
        dec_in = sem("dec_in")
        dec_exp = sem("dec_exp")
        dec_tri = sem("dec_tri")
        w_ready = sem("w_ready")
        y_mm = sem("y_mm")
        gs_in = sem("gs_in")
        gs_mm = sem("gs_mm")
        gv_ready = sem("gv_ready")
        gr_ready = sem("gr_ready")
        on_ready = sem("on_ready")
        wout_mm = sem("wout_mm")

        FIRST = [(cT, "cT"), (wmod, "wmod"), (XR, "xT"), (onesm, "onesm"), (ident, "ident")]
        REST = [(wxz, "wxz"), (convp, "convp"), (wdt, "wdt"), (head8, "head8"), (featp, "featp"),
                (wbc, "wbc"), (sel8, "sel8"), (tri, "tri"), (grpm, "grpm"), (wout, "wout")]
        block = ctx.enter_context(nc.Block())

        @block.sync
        def _(sp):
            for dst, name in FIRST:
                sp.dma_start(dst[:], t[name]).then_inc(landed, 16)
            for dst, name in REST:
                sp.dma_start(dst[:], t[name]).then_inc(weights, 16)
            sp.wait_ge(landed, 16 * len(FIRST))
            sp.wait_ge(weights, 16 * len(REST))

        @block.tensor
        def _(pe):
            mm = None
            pe.wait_ge(landed, 16 * len(FIRST))
            pe.wait_ge(silu_c, 1)
            for blk in range(2):
                for k in range(6):
                    n = (blk * 6 + k) * B
                    mm = pe.matmul(PS[:, 7, n:n + B], wmod[:, blk, k * D:(k + 1) * D], sc[:, blk, :],
                                   start=True, stop=True)
            mm.then_inc(mod_mm, 1)
            pe.wait_ge(mod_ready, 1)
            pe.wait_ge(weights, 16 * len(REST))

            def layernorm(b, k, src):
                pe.matmul(PS[:, 0, :], onesm[:], src, start=True, stop=True).then_inc(ln_mean, 1)
                pe.wait_ge(ln_sq, b * 2 + k + 1)
                pe.matmul(PS[:, 1, :], onesm[:], lnsq[:], start=True, stop=True).then_inc(ln_var, 1)

            with pe.Fori(0, B) as b:
                pe.wait_ge(a_done, b + 1)
                layernorm(b, 0, XR[:, b, :])
                pe.wait_ge(h_ready, b * 2 + 1)
                for k in range(2):
                    for m in range(FM):
                        pe.matmul(PS[:, 2 + 2 * k + m, :], wxz[:, k, m * P:(m + 1) * P], hT[:],
                                  start=True, stop=True).then_inc(xz_mm, 1)
                pe.wait_ge(xc_ready, FM * b + FM)
                for m in range(FM):
                    mm = pe.matmul(PS[0:SH, 6, :], wdt[:, m, :], xc[:, m, :], start=(m == 0), stop=(m == FM - 1))
                mm.then_inc(dt_mm, 1)
                for i in range(NT):
                    for m in range(FM):
                        mm = pe.transpose(PS[:, i // 2, (i % 2) * INNER + m * P:(i % 2) * INNER + (m + 1) * P],
                                          xc[:, m, i * P:(i + 1) * P], ident[:])
                mm.then_inc(xtok_tr, 1)
                for n in range(2 * PAIRS):
                    which, m = n // PAIRS, n % PAIRS
                    if n < 2:
                        pe.wait_ge(xpad_ready, FM * b + FM)
                    elif n < 4:
                        pe.wait_ge(zs_ready, FM * b + FM)
                    else:
                        pe.wait_ge(bc_ready, 2 * PAIRS * b + n - 3)
                    for k in range(FM):
                        mm = pe.matmul(PS[:, 2 + n % 4, :], wbc[:, which, k, m * P:(m + 1) * P], xc[:, k, :],
                                       start=(k == 0), stop=(k == FM - 1))
                    mm.then_inc(bc_mm, 1)
                pe.wait_ge(acum_ready, b + 1)
                for q in range(2):
                    for i in range(NT):
                        n = (q * NT + i) * SH
                        mm = pe.matmul(PS[:, 6, n:n + SH], d8[:, 4 + 2 * q, i * P:(i + 1) * P], ident[0:SH, 0:SH],
                                       start=True, stop=True)
                mm.then_inc(col_tr, 1)
                pe.wait_ge(xdt_ready, b + 1)

                def outputs(g):
                    m, i = g // NT, g % NT
                    pe.wait_ge(w_ready, STEPS_A * b + g + 1)
                    for q in range(2):
                        h = 2 * m + q
                        r = SP * (h % 4)
                        mm = pe.matmul(PS[r:r + SP, 6 + h // 4, i * P:L], xdt[:, i, h * SP:(h + 1) * SP],
                                       wgt[:, g % 2, q, 0:L - i * P], start=(i == 0), stop=(i == NT - 1),
                                       tile_position=(0, r))
                    mm.then_inc(y_mm, 1)

                for g in range(STEPS_A):
                    m, i = g // NT, g % NT
                    if i == 0:
                        if m:
                            pe.wait_ge(dec_in, STEPS_A * b + g)
                        for q in range(2):
                            mm = pe.matmul(PS[:, q, :], sel8[:, 2 * m + q, :], d8[:, 6, :], start=True, stop=True)
                        mm.then_inc(ab_mm, 1)
                    if g < 2:
                        pe.wait_ge(bc_ready, 2 * PAIRS * b + 2 * PAIRS)
                    else:
                        pe.wait_ge(w_ready, STEPS_A * b + g - 1)
                    for q in range(2):
                        mm = pe.matmul(PS[:, 2 + 2 * (g % 2) + q, 0:L - i * P],
                                       bcT[q * SN:(q + 1) * SN, 0, m, i * P:(i + 1) * P],
                                       bcT[q * SN:(q + 1) * SN, 1, m, i * P:L], start=True, stop=True)
                    mm.then_inc(g_mm, 1)
                    if g:
                        outputs(g - 1)
                outputs(STEPS_A - 1)
                pe.wait_ge(gs_in, b + 1)
                pe.matmul(PS[:, 2, 0:2 * FM], grpm[:], gst[:].rearrange("p a b -> p (a b)"),
                          start=True, stop=True).then_inc(gs_mm, 1)
                pe.wait_ge(on_ready, b + 1)
                for m in range(FM):
                    mm = pe.matmul(PS[:, 3, :], wout[:, m, :], onorm[:, m, :], start=(m == 0), stop=(m == FM - 1))
                mm.then_inc(wout_mm, 1)
                pe.wait_ge(ln_in, b + 1)
                layernorm(b, 1, XR[:, b, :])

        @block.scalar
        def _(act):
            st = Steps(act, act_steps)
            act.wait_ge(landed, 16 * len(FIRST))
            act.activation(sc[:], cT[:], ACT.Silu).then_inc(silu_c, 1)
            act.wait_ge(zeroed, 1)
            act.wait_ge(weights, 16 * len(REST))
            st.did(act.activation(neg_a[:, 0:1], head8[:, 1:2], ACT.Exp))

            def layernorm(b, k):
                act.wait_ge(ln_cent, b * 2 + k + 1)
                act.activation(lnsq[:], lnc[:], ACT.Square).then_inc(ln_sq, 1)
                act.wait_ge(ln_var, b * 2 + k + 1)
                st.did(act.activation(lnv[:], PS[:, 1, :], ACT.Ln, bias=epsc[:, 0:1]))
                st.wait()
                act.activation(lnr[:], lnv[:], ACT.Exp, scale=-0.5).then_inc(ln_rstd, 1)

            PER = 3
            with act.Fori(0, B) as b:
                st.enter(b, PER)
                layernorm(b, 0)
                for m in range(FM):
                    act.wait_ge(xz_mm, 2 * FM * b + m + 1)
                    act.activation(xpad[:, m, TAPS - 1:TAPS - 1 + L], PS[:, 2 + m, :], ACT.Copy).then_inc(xpad_ready, 1)
                for m in range(FM):
                    act.wait_ge(xz_mm, 2 * FM * b + FM + m + 1)
                    act.activation(zs[:, m, :], PS[:, 4 + m, :], ACT.Silu).then_inc(zs_ready, 1)
                for m in range(FM):
                    act.wait_ge(conv_ready, FM * b + m + 1)
                    act.activation(xc[:, m, :], cacc[:, m, TAPS - 1, :], ACT.Silu,
                                   bias=convp[:, m, TAPS:TAPS + 1]).then_inc(xc_ready, 1)
                act.wait_ge(dt_na, b + 1)
                st.did(act.activation(d8[:, 2, :], d8[:, 2, :], ACT.Exp))
                st.wait()
                act.activation(d8[:, 3, :], d8[:, 2, :], ACT.Ln, bias=epsc[0:SH, 1:2]).then_inc(dt_ln, 1)
                for n in range(2 * PAIRS):
                    act.wait_ge(bc_mm, 2 * PAIRS * b + n + 1)
                    act.activation(bcT[:, n // PAIRS, n % PAIRS, :], PS[:, 2 + n % 4, :], ACT.Copy).then_inc(bc_ready, 1)
                for g in range(STEPS_A):
                    n = L - (g % NT) * P
                    act.wait_ge(dec_in, STEPS_A * b + g + 1)
                    act.activation(dec[:, g % 2, :, 0:n], dec[:, g % 2, :, 0:n], ACT.Exp).then_inc(dec_exp, 1)
                layernorm(b, 1)
                st.leave(B, PER)

        @block.gpsimd
        def _(pool):
            pool.memset(xpad[:, :, 0:TAPS - 1], 0.0)
            pool.memset(mhalf[:], -0.5)
            pool.memset(d8[:, 7, :], 0.0)
            pool.memset(X[:, :, 0:PADX], 0.0)
            pool.memset(epsc[:, 0:1], EPS)
            pool.memset(epsc[:, 1:2], 1.0)
            pool.memset(XA[:, :, 0:1], 0.0).then_inc(zeroed, 1)
            pool.wait_ge(zeroed, 1)
            pool.wait_ge(weights, 16 * len(REST))
            with pool.Fori(0, B) as b:
                for g in range(STEPS_A):
                    pool.wait_ge(dec_exp, STEPS_A * b + g + 1)
                    pool.tensor_tensor(dec[:, g % 2, :, 0:P], dec[:, g % 2, :, 0:P],
                                       tri[:].unsqueeze(1).to_broadcast([P, 2, P]), ALU.mult).then_inc(dec_tri, 1)
                pool.wait_ge(gv_ready, b + 1)
                pool.tensor_tensor(gv[:, 2, :], gv[:, 1, :], mhalf[:], ALU.pow).then_inc(gr_ready, 1)

        @block.vector
        def _(v):
            st = Steps(v, dve_steps)

            def link(ins):
                st.did(ins)
                st.wait()

            v.wait_ge(mod_mm, 1)
            link(v.tensor_copy(mod[:].rearrange("p a k b -> p (a k b)"), PS[:, 7, 0:12 * B]))
            for blk in range(2):
                for k in (1, 4):
                    st.did(v.tensor_scalar(mod[:, blk, k, :], mod[:, blk, k, :], 1.0, None, ALU.add))
                for j, k in enumerate((2, 5)):
                    g = mod[:, blk, k, :]
                    n = blk * 2 + j
                    st.did(v.tensor_scalar(gtmp[:, 0, n, :], g, 0.0, 2.0, ALU.is_ge, ALU.mult))
                    st.did(v.tensor_scalar(gtmp[:, 1, n, :], g, -1.0, None, ALU.mult))
                    st.wait()
                    st.did(v.tensor_tensor(gtmp[:, 2, n, :], gtmp[:, 1, n, :], g, ALU.max))
                    st.wait()
                    st.did(v.tensor_scalar(gtmp[:, 2, n, :], gtmp[:, 2, n, :], GATE_MIN, None, ALU.max))
                    st.did(v.tensor_scalar(gtmp[:, 3, n, :], gtmp[:, 0, n, :], 1.0, None, ALU.subtract))
                    st.wait()
                    st.did(v.tensor_tensor(g, gtmp[:, 3, n, :], gtmp[:, 2, n, :], ALU.mult))
            st.wait()
            v.wait_ge(weights, 16 * len(REST))
            v.wait_ge(zeroed, 1)
            v.wait_ge(act_steps, 1)
            v.tensor_scalar(neg_a[:, 1:2], neg_a[:, 0:1], -1.0, None, ALU.mult).then_inc(mod_ready, 1)
            v.wait_ge(mod_ready, 1)
            v.sem_inc(a_done)

            def layernorm(b, k, src, scale, shift):
                v.wait_ge(ln_mean, b * 2 + k + 1)
                v.tensor_tensor(lnc[:], src, PS[:, 0, :], ALU.subtract).then_inc(ln_cent, 1)
                v.wait_ge(ln_rstd, b * 2 + k + 1)
                v.wait_ge(ln_cent, b * 2 + k + 1)
                link(v.tensor_tensor(lnt[:], lnc[:], lnr[:], ALU.mult))
                v.tensor_scalar(hT[:], lnt[:], scale, shift, ALU.mult, ALU.add).then_inc(h_ready, 1)

            PER = 33
            with v.Fori(0, B) as b:
                st.enter(b, PER)
                layernorm(b, 0, XR[:, b, :], mod[:, 0, 1, bass.ds(b, 1)], mod[:, 0, 0, bass.ds(b, 1)])
                for m in range(FM):
                    v.wait_ge(xpad_ready, FM * b + m + 1)
                    link(v.tensor_scalar(cacc[:, m, 0, :], xpad[:, m, 0:L], convp[:, m, 0:1], None, ALU.mult))
                    for k in range(1, TAPS):
                        ins = v.scalar_tensor_tensor(cacc[:, m, k, :], xpad[:, m, k:k + L], convp[:, m, k:k + 1],
                                                     cacc[:, m, k - 1, :], ALU.mult, ALU.add)
                        if k < TAPS - 1:
                            link(ins)
                        else:
                            ins.then_inc(conv_ready, 1)
                v.wait_ge(dt_mm, b + 1)
                link(v.tensor_scalar(d8[:, 0, :], PS[0:SH, 6, :], head8[:, 0:1], None, ALU.add))
                link(v.tensor_scalar(d8[:, 1, :], d8[:, 0, :], -1.0, None, ALU.mult))
                v.tensor_tensor(d8[:, 2, :], d8[:, 0, :], d8[:, 1, :], ALU.min).then_inc(dt_na, 1)
                v.wait_ge(dt_ln, b + 1)
                link(v.scalar_tensor_tensor(d8[:, 4, :], d8[:, 0, :], 0.0, d8[:, 3, :], ALU.max, ALU.add))
                link(v.tensor_scalar(d8[:, 5, :], d8[:, 4, :], neg_a[:, 1:2], None, ALU.mult))
                v.tensor_tensor_scan(d8[:, 6, :], d8[:, 5, :], d8[:, 7, :], 0.0, ALU.add, ALU.add).then_inc(acum_ready, 1)
                v.wait_ge(col_tr, b + 1)
                link(v.tensor_copy(cols[:].rearrange("p a i h -> p (a i h)"), PS[:, 6, 0:2 * NT * SH]))
                v.wait_ge(xtok_tr, b + 1)
                for k in range(2):
                    ins = v.tensor_tensor(xdt[:, 2 * k:2 * k + 2, :].rearrange("p i (h w) -> p (i h) w", w=SP),
                                          PS[:, k, :].rearrange("p (n w) -> p n w", w=SP),
                                          cols[:, 0, 2 * k:2 * k + 2, :].rearrange("p i h -> p (i h)").unsqueeze(2)
                                          .to_broadcast([P, 2 * SH, SP]), ALU.mult)
                ins.then_inc(xdt_ready, 1)

                def weigh(g):
                    n = L - (g % NT) * P
                    v.wait_ge(dec_tri, STEPS_A * b + g + 1)
                    v.wait_ge(g_mm, STEPS_A * b + g + 1)
                    if g >= 2:
                        v.wait_ge(y_mm, STEPS_A * b + g - 1)
                    k = 2 + 2 * (g % 2)
                    v.tensor_tensor(wgt[:, g % 2, :, 0:n], dec[:, g % 2, :, 0:n], PS[:, k:k + 2, 0:n],
                                    ALU.mult).then_inc(w_ready, 1)

                for g in range(STEPS_A):
                    m, i = g // NT, g % NT
                    if i == 0:
                        v.wait_ge(ab_mm, PAIRS * b + m + 1)
                    if g >= 2:
                        v.wait_ge(w_ready, STEPS_A * b + g - 1)
                    for q in range(2):
                        h = 2 * m + q
                        ins = v.tensor_scalar(dec[:, g % 2, q, 0:L - i * P], PS[:, q, i * P:L],
                                              cols[:, 1, i, h:h + 1], 0.0, ALU.subtract, ALU.min)
                    ins.then_inc(dec_in, 1)
                    if g:
                        weigh(g - 1)
                weigh(STEPS_A - 1)
                v.wait_ge(y_mm, STEPS_A * b + STEPS_A)
                for m in range(FM):
                    link(v.scalar_tensor_tensor(ysb[:, m, :], xc[:, m, :], featp[:, m, 0:1], PS[:, 6 + m, :],
                                                ALU.mult, ALU.add))
                    link(v.bn_stats(bst[:, m, :], ysb[:, m, :]))
                link(v.tensor_tensor(gv[:, 0, :], bst[:, :, 1], bst[:, :, 4], ALU.add))
                link(v.tensor_scalar(gst[:, 0, :], gv[:, 0, :], 0.5, None, ALU.mult))
                link(v.tensor_tensor(gv[:, 3, :], bst[:, :, 1], bst[:, :, 1], ALU.mult))
                link(v.tensor_tensor(gv[:, 4, :], bst[:, :, 4], bst[:, :, 4], ALU.mult))
                link(v.tensor_tensor(gv[:, 5, :], gv[:, 3, :], gv[:, 4, :], ALU.add))
                link(v.tensor_tensor(gv[:, 6, :], bst[:, :, 2], bst[:, :, 5], ALU.add))
                link(v.tensor_scalar(gv[:, 7, :], gv[:, 6, :], 1.0 / L, None, ALU.mult))
                ins = v.scalar_tensor_tensor(gst[:, 1, :], gv[:, 5, :], 0.5, gv[:, 7, :], ALU.mult, ALU.add)
                ins.then_inc(gs_in, 1)
                v.wait_ge(gs_mm, b + 1)
                link(v.tensor_copy(gsm[:].rearrange("p a b -> p (a b)"), PS[:, 2, 0:2 * FM]))
                link(v.tensor_tensor(gv[:, 0, :], gsm[:, 0, :], gsm[:, 0, :], ALU.mult))
                link(v.tensor_tensor(gv[:, 3, :], gsm[:, 1, :], gv[:, 0, :], ALU.subtract))
                v.tensor_scalar(gv[:, 1, :], gv[:, 3, :], 0.0, EPS, ALU.max, ALU.add).then_inc(gv_ready, 1)
                v.wait_ge(gr_ready, b + 1)
                link(v.tensor_tensor(gv[:, 4, :], gv[:, 2, :], featp[:, :, 1], ALU.mult))
                link(v.tensor_tensor(gv[:, 5, :], gsm[:, 0, :], gv[:, 4, :], ALU.mult))
                link(v.tensor_tensor(gv[:, 6, :], featp[:, :, 2], gv[:, 5, :], ALU.subtract))
                v.wait_ge(zs_ready, FM * b + FM)
                for m in range(FM):
                    link(v.tensor_scalar(yn[:, m, :], ysb[:, m, :], gv[:, 4, m:m + 1], gv[:, 6, m:m + 1],
                                         ALU.mult, ALU.add))
                    ins = v.tensor_tensor(onorm[:, m, :], yn[:, m, :], zs[:, m, :], ALU.mult)
                ins.then_inc(on_ready, 1)
                v.wait_ge(wout_mm, b + 1)
                v.scalar_tensor_tensor(XR[:, b, :], PS[:, 3, :], mod[:, 0, 2, bass.ds(b, 1)], XR[:, b, :],
                                       ALU.mult, ALU.add).then_inc(ln_in, 1)
                v.wait_ge(ln_in, b + 1)
                layernorm(b, 1, XR[:, b, :], mod[:, 0, 4, bass.ds(b, 1)], mod[:, 0, 3, bass.ds(b, 1)])
                v.wait_ge(h_ready, 2 * b + 2)
                link(v.tensor_copy(X[:, b, PADX:PADX + L], hT[:]))
                v.tensor_copy(XA[:, b, 1:1 + L], hT[:]).then_inc(a_done, 1)
                st.leave(B, PER)
            v.wait_ge(a_done, B + 1)


def local_layers(nc, t, X, XA, PS, onesm, ident, epsc):
    with ExitStack() as ctx:
        def sb(name, shape):
            return ctx.enter_context(nc.sbuf_tensor(name, shape, F32))

        def sem(name):
            return ctx.enter_context(nc.semaphore(name))

        HW = QD // 2
        LAST = NT
        BQK, BPV, BV, BRT, BS, BPT = 0, (7, 1), 2, 3, 4, 6

        amask = sb("amask", [P, 2, GH * 2 * WIN])
        rotc = sb("rotc", [P, NT, 2, QD])
        rots = sb("rots", [P, NT, 2, QD])
        wqkv = sb("wqkv", [P, NG, 3 * GW])
        qkg = sb("qkg", [P, 2, 2, QD])
        wog = sb("wog", [P, 2, D])
        w1 = sb("w1", [P, 2 * FF])
        w2 = sb("w2", [P, FK, D])
        ffp = sb("ffp", [P, 2 * FK + 3])
        mhalf = sb("b_mhalf", [P, 2 * GH])
        xst = sb("xst", [P, NT, WIN + P])
        qk = sb("qk", [P, 2, 2, GH, QD])
        qksq = sb("qksq", [P, 2, GH, QD])
        ssr = sb("ssr", [P, 2 * GH])
        ssq = sb("ssq", [P, 2, 2 * GH])
        rn = sb("rn", [P, 2, 2 * GH])
        rc = sb("rc", [P, NT, 2, QD])
        rs = sb("rs", [P, NT, 2, QD])
        qkn = sb("qkn", [P, 2, 2, GH, QD])
        qkc = sb("qkc", [P, 2, GH, QD])
        qks = sb("qks", [P, 2, GH, QD])
        qkr = sb("qkr", [P, 2, 2, GH, QD])
        qT = sb("qT", [P, 2, 2, P])
        kT = sb("kT", [P, 2, WIN + L])
        vab = sb("vab", [P, NT, 2, GW])
        sm = sb("sm", [P, GH, 2 * WIN])
        smx = sb("smx", [P, GH])
        smd = sb("smd", [P, 2, GH, 2 * WIN])
        pex = sb("pex", [P, 2, GH, 2 * WIN])
        zsum = sb("zsum", [P, GH])
        zinv = sb("zinv", [P, GH])
        pn = sb("pn", [P, 2, GH, 2, 2 * WIN])
        pT = sb("pT", [P, 2, GH, 2 * WIN])
        oT = sb("oT", [P, 2, L])
        fx = sb("fx", [P, 2, L])
        fc = sb("fc", [P, 2, L])
        fsq = sb("fsq", [P, L])
        flv = sb("flv", [P, L])
        frs = sb("frs", [P, 2, L])
        fn = sb("fn", [P, L])
        fh = sb("fh", [P, 2, L])
        fg = sb("fg", [P, FK, L])
        fa = sb("fa", [P, FK, L])

        tables = sem("b_tables")
        zeroed = sem("b_zeroed")
        xst_in = [sem(f"xst_in{i}") for i in range(NT)]
        w_in = sem("w_in")
        wo_in = sem("wo_in")
        ffw_in = sem("ffw_in")
        scaled = sem("scaled")
        qk_mm = sem("qk_mm")
        v_mm = sem("v_mm")
        qk_out = sem("qk_out")
        v_out = sem("v_out")
        sq_sum = sem("sq_sum")
        sq_ready = sem("sq_ready")
        rn_ready = sem("rn_ready")
        n_ready = sem("n_ready")
        cos_done = sem("cos_done")
        sin_done = sem("sin_done")
        r_ready = sem("r_ready")
        rt_tr = sem("rt_tr")
        rt_out = sem("rt_out")
        s_mm = sem("s_mm")
        s_out = sem("s_out")
        mx_ready = sem("mx_ready")
        d_ready = sem("d_ready")
        e_ready = sem("e_ready")
        z_ready = sem("z_ready")
        zi_ready = sem("zi_ready")
        p_ready = sem("p_ready")
        pt_tr = sem("pt_tr")
        pt_out = sem("pt_out")
        pv_mm = sem("pv_mm")
        pv_out = sem("pv_out")
        wo_mm = sem("wo_mm")
        passed = sem("passed")
        att_done = sem("att_done")
        ff_x = sem("ff_x")
        ff_mean = sem("ff_mean")
        ff_c = sem("ff_c")
        ff_sq = sem("ff_sq")
        ff_var = sem("ff_var")
        ff_lv = sem("ff_lv")
        ff_rs = sem("ff_rs")
        ff_n = sem("ff_n")
        ff_h = sem("ff_h")
        ff_gm = sem("ff_gm")
        ff_g = sem("ff_g")
        ff_am = sem("ff_am")
        ff_a = sem("ff_a")
        ff_ym = sem("ff_ym")
        ff_new = sem("ff_new")
        ff_done = sem("ff_done")

        def stage(s, it, lag):
            d = s - lag
            w = it + d // NT
            return d % NT, w, not isinstance(it, int) or 0 <= w < PASSES

        def layers(eng, step, before=None, after=None):
            with eng.Fori(0, DEPTH) as l:
                if before:
                    before(l)
                for s in range(NT):
                    step(l, 0, s)
                with eng.Fori(1, PASSES) as it:
                    for s in range(NT):
                        step(l, it, s)
                for s in range(LAST):
                    step(l, PASSES, s)
                if after:
                    after(l)

        def units(l, w, tile):
            return l * UNITS + w * NT + (tile + 1)

        def first(w, tile, n=1):
            return isinstance(w, int) and w * NT + tile < n

        block = ctx.enter_context(nc.Block())

        @block.sync
        def _(sp):
            for dst, name in ((amask, "amask"), (rotc, "rotc"), (rots, "rots")):
                sp.dma_start(dst[:], t[name]).then_inc(tables, 16)

            def load_x(l, w, tile):
                if not first(w, tile, NT):
                    sp.wait_ge(v_mm, 1 + units(l, w, tile) - NT)
                b = w % B
                lo = tile * P
                sp.dma_start(xst[0:HALF, tile, :], X[0:HALF, b, lo + 1:lo + 1 + WIN + P]).then_inc(xst_in[tile], 16)
                sp.dma_start(xst[HALF:P, tile, :], X[HALF:P, b, lo:lo + WIN + P]).then_inc(xst_in[tile], 16)

            def load_wo(l, w):
                sp.wait_ge(wo_mm, 1 + l * PASSES + w)
                sp.dma_start(wog[:], t["wo"][l, w // B]).then_inc(wo_in, 16)

            HALF = D // 2
            with sp.Fori(0, DEPTH) as l:
                sp.wait_ge(v_mm, 1 + l * UNITS)
                sp.dma_start(wqkv[:], t["wqkv"][l]).then_inc(w_in, 16)
                sp.wait_ge(scaled, 1 + 2 * l)
                sp.dma_start(qkg[:], t["qkg"][l]).then_inc(w_in, 16)
                sp.wait_ge(ff_done, 1 + B * l)
                sp.dma_start(w1[:], t["w1"][l]).then_inc(ffw_in, 16)
                sp.dma_start(w2[:], t["w2"][l]).then_inc(ffw_in, 16)
                sp.dma_start(ffp[:], t["ffp"][l]).then_inc(ffw_in, 16)
                for tile in range(NT):
                    load_x(l, 0, tile)
                load_wo(l, 0)
                with sp.Fori(1, PASSES) as w:
                    for tile in range(NT):
                        load_x(l, w, tile)
                    load_wo(l, w)
            sp.wait_ge(tables, 48)

        @block.tensor
        def _(pe):
            def rotated_T(l, w, tile):
                pe.wait_ge(r_ready, units(l, w, tile))
                if not first(w, tile):
                    pe.wait_ge(rt_out, units(l, w, tile) - 1)
                for k in range(4):
                    mm = pe.transpose(PS[:, BRT, k * P:(k + 1) * P],
                                      qkr[:, tile % 2, k // 2, (k % 2) * 2:(k % 2) * 2 + 2, :]
                                      .rearrange("p h d -> p (h d)"), ident[:])
                mm.then_inc(rt_tr, 1)

            def project_qk(l, w, tile):
                pe.wait_ge(xst_in[tile], 32 * (l * PASSES + w + 1))
                if not first(w, tile):
                    pe.wait_ge(qk_out, units(l, w, tile) - 1)
                pe.matmul(PS[:, BQK, :], xst[:, tile, WIN:WIN + P], wqkv[:, w // B, 0:2 * GW],
                          start=True, stop=True).then_inc(qk_mm, 1)

            def project_v(l, w, tile):
                if not first(w, tile):
                    pe.wait_ge(v_out, units(l, w, tile) - 1)
                if tile == 0 and not (isinstance(w, int) and w < 2):
                    pe.wait_ge(att_done, 1 + l * PASSES + w - 1)
                for k in range(2):
                    mm = pe.matmul(PS[:, BV, k * GW:(k + 1) * GW], xst[:, tile, WIN * (1 - k):WIN * (1 - k) + P],
                                   wqkv[:, w // B, 2 * GW:3 * GW], start=True, stop=True)
                mm.then_inc(v_mm, 1)

            def probs_T(l, w, tile):
                pe.wait_ge(p_ready, units(l, w, tile))
                if not first(w, tile):
                    pe.wait_ge(pt_out, units(l, w, tile) - 1)
                for k in range(GH):
                    mm = pe.transpose(PS[:, BPT, k * P:(k + 1) * P],
                                      pn[:, tile % 2, k, :, :].rearrange("p a k -> p (a k)"), ident[:])
                mm.then_inc(pt_tr, 1)

            def scores(l, w, tile):
                pe.wait_ge(rt_out, units(l, w, tile))
                if not first(w, tile):
                    pe.wait_ge(s_out, units(l, w, tile) - 1)
                pe.sem_inc(passed)
                for j in range(NW):
                    for e in range(GH):
                        r = QD * (e % 2)
                        mm = pe.matmul(PS[WIN * j:WIN * (j + 1), BS + e % 2, 2 * WIN * (e // 2):2 * WIN * (e // 2 + 1)],
                                       qT[r:r + QD, tile % 2, e // 2, WIN * j:WIN * (j + 1)],
                                       kT[r:r + QD, e // 2, tile * P + WIN * j:tile * P + WIN * (j + 2)],
                                       start=True, stop=True)
                mm.then_inc(s_mm, 1)

            def times_v(l, w, tile):
                pe.wait_ge(pt_out, units(l, w, tile))
                pe.wait_ge(v_out, units(l, w, tile))
                if not first(w, tile):
                    pe.wait_ge(pv_out, units(l, w, tile) - 1)
                pe.sem_inc(passed)
                for jj in range(2):
                    for e in range(GH):
                        for half in range(2):
                            r, o = QD * half, QD * (e % 2)
                            mm = pe.matmul(PS[o:o + QD, BPV[half], (e // 2) * 2 * WIN + jj * WIN:(e // 2) * 2 * WIN + (jj + 1) * WIN],
                                           vab[r:r + QD, tile, 1 - jj, e * QD:(e + 1) * QD],
                                           pT[r:r + QD, tile % 2, (e % 2) * 2 + e // 2, jj * WIN:(jj + 1) * WIN],
                                           start=True, stop=True)
                mm.then_inc(pv_mm, 1)

            def output(l, w):
                pe.wait_ge(wo_in, 16 * (l * PASSES + w + 1))
                pe.wait_ge(pv_out, units(l, w, NT - 1))
                pe.wait_ge(v_out, l * UNITS + UNITS if isinstance(w, int) and w == PASSES - 1
                           else units(l, w + 1, NT - 1))
                for k in range(2):
                    mm = pe.matmul(PS[:, BV, :], wog[:, k, :], oT[:, k, :], start=(k == 0), stop=(k == 1))
                mm.then_inc(wo_mm, 1)

            def step(l, it, s):
                tile2, w2_, live2 = stage(s, it, 2)
                tile3, w3, live3 = stage(s, it, 3)
                tile0, w0, live0 = stage(s, it, 0)
                tile4, w4, live4 = stage(s, it, LAST)
                if live2:
                    rotated_T(l, w2_, tile2)
                if live0:
                    project_qk(l, w0, tile0)
                    project_v(l, w0, tile0)
                if live3:
                    probs_T(l, w3, tile3)
                if live2:
                    scores(l, w2_, tile2)
                if live4 and tile4 == NT - 1:
                    output(l, w4)
                if live3:
                    times_v(l, w3, tile3)

            def before(l):
                pe.wait_ge(w_in, 32 * (l + 1))

            def ffn(l):
                def mean(b):
                    pe.wait_ge(ff_x, l * B + b + 1)
                    pe.matmul(PS[:, 0, :], onesm[:], fx[:, b % 2, :], start=True, stop=True).then_inc(ff_mean, 1)

                def var(b):
                    pe.wait_ge(ff_sq, l * B + b + 1)
                    pe.matmul(PS[:, 1, :], onesm[:], fsq[:], start=True, stop=True).then_inc(ff_var, 1)

                pe.wait_ge(ffw_in, 48 * (l + 1))
                mean(0)
                var(0)
                for b in range(B):
                    pe.wait_ge(ff_h, l * B + b + 1)
                    for r in range(FK):
                        if b and r == 0:
                            pe.wait_ge(ff_a, (l * B + b) * FK)
                        pe.matmul(PS[0:FR[r], 3 + r, :], w1[:, FF + r * P:FF + r * P + FR[r]], fh[:, b % 2, :],
                                  start=True, stop=True).then_inc(ff_gm, 1)
                    if b + 1 < B:
                        mean(b + 1)
                    for r in range(FK):
                        if r == 2:
                            pe.wait_ge(ff_g, (l * B + b) * FK + 1)
                        pe.matmul(PS[0:FR[r], (6, 7, 3)[r], :], w1[:, r * P:r * P + FR[r]], fh[:, b % 2, :],
                                  start=True, stop=True).then_inc(ff_am, 1)
                    if b + 1 < B:
                        var(b + 1)
                    if b:
                        pe.wait_ge(ff_new, l * B + b)
                    for r in range(FK):
                        pe.wait_ge(ff_a, (l * B + b) * FK + r + 1)
                        mm = pe.matmul(PS[:, 2, :], w2[0:FR[r], r, :], fa[0:FR[r], r, :],
                                       start=(r == 0), stop=(r == FK - 1))
                    mm.then_inc(ff_ym, 1)

            pe.wait_ge(zeroed, 1)
            for credit in (v_mm, wo_mm):
                pe.sem_inc(credit)
            layers(pe, step, before, ffn)

        @block.scalar
        def _(act):
            def exps(l, w, tile):
                act.wait_ge(d_ready, units(l, w, tile))
                act.activation(pex[:, tile % 2], smd[:, tile % 2], ACT.Exp).then_inc(e_ready, 1)

            def rotated_out(l, w, tile):
                act.wait_ge(rt_tr, units(l, w, tile))
                act.activation(qT[:, tile % 2], PS[:, BRT, 0:2 * P].rearrange("p (a n) -> p a n", a=2), ACT.Copy)
                act.activation(kT[:, :, WIN + tile * P:WIN + (tile + 1) * P],
                               PS[:, BRT, 2 * P:4 * P].rearrange("p (a n) -> p a n", a=2), ACT.Copy).then_inc(rt_out, 1)

            def qk_copy(l, w, tile):
                act.wait_ge(qk_mm, units(l, w, tile))
                if not first(w, tile):
                    act.wait_ge(sq_sum, units(l, w, tile) - 1)
                if not first(w, tile, 2):
                    act.wait_ge(n_ready, units(l, w, tile) - 2)
                act.activation(qk[:, tile % 2].rearrange("p a h d -> p (a h d)"), PS[:, BQK, :], ACT.Copy)
                act.activation(qksq[:].rearrange("p a h d -> p (a h d)"), PS[:, BQK, :], ACT.Square).then_inc(qk_out, 1)

            def probs_out(l, w, tile):
                act.wait_ge(pt_tr, units(l, w, tile))
                for half in range(2):
                    r = QD * half
                    ins = act.activation(pT[r:r + QD, tile % 2],
                                         PS[r:r + QD, BPT, :].rearrange("p (k n) -> p k n", k=GH)
                                         [:, :, half * 2 * WIN:(half + 1) * 2 * WIN], ACT.Copy)
                ins.then_inc(pt_out, 1)

            def v_copy(l, w, tile):
                act.wait_ge(v_mm, 1 + units(l, w, tile))
                act.activation(vab[:, tile].rearrange("p a n -> p (a n)"), PS[:, BV, :], ACT.Copy).then_inc(v_out, 1)

            def o_copy(l, w, tile):
                act.wait_ge(pv_mm, units(l, w, tile))
                for half in range(2):
                    lo = tile * P + half * 2 * WIN
                    ins = act.activation(oT[:, :, lo:lo + 2 * WIN],
                                         PS[:, BPV[half], 0:4 * WIN].rearrange("p (a n) -> p a n", a=2), ACT.Copy)
                ins.then_inc(pv_out, 1)

            def step(l, it, s):
                tile2, w2_, live2 = stage(s, it, 2)
                tile3, w3, live3 = stage(s, it, 3)
                tile0, w0, live0 = stage(s, it, 0)
                if live2:
                    rotated_out(l, w2_, tile2)
                if live0:
                    qk_copy(l, w0, tile0)
                    v_copy(l, w0, tile0)
                if live3:
                    probs_out(l, w3, tile3)
                    o_copy(l, w3, tile3)
                if live2:
                    exps(l, w2_, tile2)

            def ffn(l):
                def square(b):
                    act.wait_ge(ff_c, l * B + b + 1)
                    act.activation(fsq[:], fc[:, b % 2, :], ACT.Square).then_inc(ff_sq, 1)

                def rstd(b):
                    act.wait_ge(ff_var, l * B + b + 1)
                    act.activation(flv[:], PS[:, 1, :], ACT.Ln, bias=epsc[:, 0:1]).then_inc(ff_lv, 1)
                    act.wait_ge(ff_lv, l * B + b + 1)
                    act.activation(frs[:, b % 2, :], flv[:], ACT.Exp, scale=-0.5).then_inc(ff_rs, 1)

                square(0)
                rstd(0)
                for b in range(B):
                    for r in range(FK):
                        act.wait_ge(ff_gm, (l * B + b) * FK + r + 1)
                        if b:
                            act.wait_ge(ff_a, (l * B + b - 1) * FK + r + 1)
                        act.activation(fg[0:FR[r], r, :], PS[0:FR[r], 3 + r, :], ACT.Gelu,
                                       bias=ffp[0:FR[r], FK + r:FK + r + 1]).then_inc(ff_g, 1)
                    if b + 1 < B:
                        square(b + 1)
                        rstd(b + 1)

            layers(act, step, None, ffn)

        @block.gpsimd
        def _(pool):
            pool.memset(mhalf[:], -0.5)
            pool.memset(kT[:, :, 0:WIN], 0.0).then_inc(zeroed, 1)
            pool.wait_ge(zeroed, 1)

            def sines(l, w, tile):
                pool.wait_ge(n_ready, units(l, w, tile))
                if not first(w, tile):
                    pool.wait_ge(r_ready, units(l, w, tile) - 1)
                for half in range(2):
                    a, c = half * HW, (1 - half) * HW
                    ins = pool.tensor_tensor(qks[:, :, :, a:a + HW], qkn[:, tile % 2, :, :, c:c + HW],
                                             rs[:, tile, :, a:a + HW].unsqueeze(2).to_broadcast([P, 2, GH, HW]),
                                             ALU.mult)
                ins.then_inc(sin_done, 1)

            def inverse_norms(l, w, tile):
                pool.wait_ge(sq_ready, units(l, w, tile))
                pool.tensor_tensor(rn[:, tile % 2, :], ssq[:, tile % 2, :], mhalf[:], ALU.pow).then_inc(rn_ready, 1)

            def step(l, it, s):
                tile1, w1_, live1 = stage(s, it, 1)
                tile0, w0, live0 = stage(s, it, 0)
                if live1:
                    sines(l, w1_, tile1)
                if live0:
                    inverse_norms(l, w0, tile0)

            def before(l):
                pool.wait_ge(scaled, 1 + 2 * l + 2)

            layers(pool, step, before)

        @block.vector
        def _(v):
            def normalise(l, w, tile):
                v.wait_ge(e_ready, units(l, w, tile))
                v.tensor_reduce(zsum[:], pex[:, tile % 2], AX.X, ALU.add).then_inc(z_ready, 1)
                v.wait_ge(z_ready, units(l, w, tile))
                v.reciprocal(zinv[:], zsum[:]).then_inc(zi_ready, 1)
                v.wait_ge(zi_ready, units(l, w, tile))
                v.tensor_tensor(pn[:, tile % 2], pex[:, tile % 2].unsqueeze(2).to_broadcast([P, GH, 2, 2 * WIN]),
                                zinv[:].unsqueeze(2).unsqueeze(3).to_broadcast([P, GH, 2, 2 * WIN]),
                                ALU.mult).then_inc(p_ready, 1)

            def rotate_1(l, w, tile):
                v.wait_ge(rn_ready, units(l, w, tile))
                if not first(w, tile, 2):
                    v.wait_ge(sin_done, units(l, w, tile) - 2)
                v.tensor_tensor(qkn[:, tile % 2].rearrange("p a h d -> p (a h) d"),
                                qk[:, tile % 2].rearrange("p a h d -> p (a h) d"),
                                rn[:, tile % 2, :].unsqueeze(2).to_broadcast([P, 2 * GH, QD]), ALU.mult).then_inc(n_ready, 1)
                v.wait_ge(n_ready, units(l, w, tile))
                v.tensor_tensor(qkc[:], qkn[:, tile % 2], rc[:, tile].unsqueeze(2).to_broadcast([P, 2, GH, QD]),
                                ALU.mult).then_inc(cos_done, 1)

            def square_sums(l, w, tile):
                v.wait_ge(qk_out, units(l, w, tile))
                v.tensor_reduce(ssr[:], qksq[:].rearrange("p a h d -> p (a h) d"), AX.X, ALU.add).then_inc(sq_sum, 1)
                v.wait_ge(sq_sum, units(l, w, tile))
                v.tensor_scalar(ssq[:, tile % 2, :], ssr[:], NORM_MIN * NORM_MIN, None, ALU.max).then_inc(sq_ready, 1)

            def rotate_2(l, w, tile):
                v.wait_ge(sin_done, units(l, w, tile))
                v.wait_ge(cos_done, units(l, w, tile))
                v.tensor_tensor(qkr[:, tile % 2], qkc[:], qks[:], ALU.add).then_inc(r_ready, 1)

            def softmax_1(l, w, tile):
                v.wait_ge(s_mm, units(l, w, tile))
                k = 0 if tile == 0 else 1
                v.scalar_tensor_tensor(sm[:].rearrange("p (a c) n -> p a (c n)", a=2), PS[:, BS:BS + 2, 0:4 * WIN],
                                       QK_SCALE, amask[:, k].rearrange("p (a n) -> p a n", a=2),
                                       ALU.mult, ALU.add).then_inc(s_out, 1)
                v.wait_ge(s_out, units(l, w, tile))
                v.tensor_reduce(smx[:], sm[:], AX.X, ALU.max).then_inc(mx_ready, 1)
                v.wait_ge(mx_ready, units(l, w, tile))
                v.tensor_tensor(smd[:, tile % 2], sm[:], smx[:].unsqueeze(2).to_broadcast([P, GH, 2 * WIN]),
                                ALU.subtract).then_inc(d_ready, 1)

            def add_output(l, w):
                v.wait_ge(wo_mm, 1 + l * PASSES + w + 1)
                xa = XA[:, w % B, 1:1 + L]
                v.tensor_tensor(xa, PS[:, BV, :], xa, ALU.add).then_inc(att_done, 1)

            def step(l, it, s):
                tile1, w1_, live1 = stage(s, it, 1)
                tile2, w2_, live2 = stage(s, it, 2)
                tile3, w3, live3 = stage(s, it, 3)
                tile0, w0, live0 = stage(s, it, 0)
                tile4, w4, live4 = stage(s, it, LAST)
                if live3:
                    normalise(l, w3, tile3)
                if live1:
                    rotate_1(l, w1_, tile1)
                if live0:
                    square_sums(l, w0, tile0)
                if live1:
                    rotate_2(l, w1_, tile1)
                if live2:
                    softmax_1(l, w2_, tile2)
                if live4 and tile4 == NT - 1:
                    add_output(l, w4)

            def before(l):
                v.wait_ge(w_in, 32 * (l + 1))
                for dst, src, k in ((rc, rotc, 0), (rs, rots, 1)):
                    v.tensor_tensor(dst[:], src[:], qkg[:, k].unsqueeze(1).to_broadcast([P, NT, 2, QD]),
                                    ALU.mult).then_inc(scaled, 1)
                v.wait_ge(scaled, 1 + 2 * l + 2)

            def ffn(l):
                def shift(b):
                    v.tensor_copy(fx[0:D // 2, b % 2, :], XA[0:D // 2, b, 1:1 + L])
                    v.tensor_copy(fx[D // 2:D, b % 2, :], XA[D // 2:D, b, 0:L]).then_inc(ff_x, 1)

                def centre(b):
                    v.wait_ge(ff_mean, l * B + b + 1)
                    v.wait_ge(ff_x, l * B + b + 1)
                    v.tensor_tensor(fc[:, b % 2, :], fx[:, b % 2, :], PS[:, 0, :], ALU.subtract).then_inc(ff_c, 1)

                def scale(b):
                    v.wait_ge(ff_rs, l * B + b + 1)
                    v.wait_ge(ff_c, l * B + b + 1)
                    v.tensor_tensor(fn[:], fc[:, b % 2, :], frs[:, b % 2, :], ALU.mult).then_inc(ff_n, 1)
                    v.wait_ge(ff_n, l * B + b + 1)
                    v.tensor_scalar(fh[:, b % 2, :], fn[:], ffp[:, 2 * FK + 1:2 * FK + 2], ffp[:, 2 * FK + 2:2 * FK + 3],
                                    ALU.mult, ALU.add).then_inc(ff_h, 1)

                v.wait_ge(att_done, 1 + PASSES * (l + 1))
                v.wait_ge(ffw_in, 48 * (l + 1))
                shift(0)
                centre(0)
                scale(0)
                for b in range(B):
                    if b + 1 < B:
                        shift(b + 1)
                        centre(b + 1)
                    for r in range(FK):
                        v.wait_ge(ff_am, (l * B + b) * FK + r + 1)
                        v.wait_ge(ff_g, (l * B + b) * FK + r + 1)
                        v.scalar_tensor_tensor(fa[0:FR[r], r, :], PS[0:FR[r], (6, 7, 3)[r], :], ffp[0:FR[r], r:r + 1],
                                               fg[0:FR[r], r, :], ALU.add, ALU.mult).then_inc(ff_a, 1)
                    if b + 1 < B:
                        scale(b + 1)
                    v.wait_ge(ff_ym, l * B + b + 1)
                    v.scalar_tensor_tensor(X[:, b, PADX:PADX + L], PS[:, 2, :], ffp[:, 2 * FK:2 * FK + 1],
                                           XA[:, b, 1:1 + L], ALU.add, ALU.add).then_inc(ff_new, 1)
                    v.wait_ge(ff_new, l * B + b + 1)
                    v.tensor_copy(XA[:, b, 1:1 + L], X[:, b, PADX:PADX + L]).then_inc(ff_done, 1)
                v.wait_ge(ff_done, 1 + B * (l + 1))

            v.wait_ge(tables, 48)
            for credit in (scaled, att_done, ff_done):
                v.sem_inc(credit)
            layers(v, step, before, ffn)


def attention_and_experts(nc, t, XR, X, mod, PS, onesm, ident, epsc, sel8, out):
    with ExitStack() as ctx:
        def sb(name, shape):
            return ctx.enter_context(nc.sbuf_tensor(name, shape, F32))

        def sem(name):
            return ctx.enter_context(nc.semaphore(name))

        PAIR = AH // 2
        NP = NT * PAIR
        aq = sb("aq", [P, AH * AD])
        akd = sb("akd", [P, AR])
        akv = sb("akv", [AR, 2, AH * AD])
        awo = sb("awo", [P, 2, D])
        rw = sb("rw", [P, NE])
        rb = sb("rb", [P, NE])
        ridx = sb("ridx", [P, NE])
        sw13 = sb("sw13", [P, 2, 2 * P])
        sw2 = sb("sw2", [P, 2, D])
        ew1 = sb("ew1", [P, NE, P])
        ew2 = sb("ew2", [P, NE, D])
        lnc = sb("c_lnc", [P, L])
        lnsq = sb("c_lnsq", [P, L])
        lnv = sb("c_lnv", [P, L])
        lnr = sb("c_lnr", [P, L])
        lnt = sb("c_lnt", [P, L])
        hT = sb("c_hT", [P, L])
        qT = sb("c_qT", [P, 2, L])
        kT = sb("c_kT", [P, 2, L])
        lat = sb("c_lat", [AR, L])
        vt = sb("c_v", [P, NT, AH * AD])
        amx = sb("amx", [P, 2, 2])
        anm = sb("anm", [P, 2, 2])
        prob = sb("prob", [P, 4, L])
        probT = sb("probT", [P, 2, NT, P])
        asum = sb("asum", [P, NT, AH])
        arz = sb("arz", [P, NT, AH])
        aon = sb("aon", [P, NT, AH * AD])
        aoT = sb("aoT", [P, 2, L])
        rsg = sb("rsg", [P, NT, NE])
        rt = sb("rt", [P, 10, NT, NE])
        rm = sb("rm", [P, 12, NT])
        comb = sb("comb", [P, NT, NE])
        combT = sb("combT", [NE, L])
        shs = sb("shs", [P, 2, L])
        shg = sb("shg", [P, 2, L])
        eh = sb("eh", [P, 2, L])
        eg = sb("eg", [P, 2, L])
        res = sb("res", [P, L])

        weights = sem("c_weights")
        dve_steps = sem("c_dve_steps")
        ln_in = sem("c_ln_in")
        ln_mean = sem("c_ln_mean")
        ln_cent = sem("c_ln_cent")
        ln_sq = sem("c_ln_sq")
        ln_var = sem("c_ln_var")
        ln_lv = sem("c_ln_lv")
        ln_rstd = sem("c_ln_rstd")
        h_ready = sem("c_h_ready")
        prj_mm = sem("prj_mm")
        prj_out = sem("prj_out")
        sc_mm = sem("sc_mm")
        max_in = sem("max_in")
        max_ready = sem("max_ready")
        prob_ready = sem("prob_ready")
        pt_tr = sem("c_pt_tr")
        pt_out = [sem("pt_out_dve"), sem("pt_out_act")]
        o_mm = sem("o_mm")
        rz_ready = sem("rz_ready")
        on_ready = sem("c_on_ready")
        ot_tr = sem("ot_tr")
        ot_out = sem("ot_out")
        ay_mm = sem("ay_mm")
        rt_mm = sem("rt_mm")
        sig_ready = sem("sig_ready")
        comb_ready = sem("comb_ready")
        ct_tr = sem("ct_tr")
        ct_out = sem("ct_out")
        sh_mm = sem("sh_mm")
        sh_silu = sem("sh_silu")
        sh_ready = sem("sh_ready")
        eh_mm = sem("eh_mm")
        cb_mm = sem("cb_mm")
        eh_ready = sem("eh_ready")
        eg_ready = sem("eg_ready")
        ey_mm = sem("ey_mm")
        last_mm = sem("last_mm")
        res_ready = sem("res_ready")
        stored = sem("stored")

        WEIGHTS = [(aq, "aq"), (akd, "akd"), (akv, "akv"), (awo, "awo"), (rw, "rw"), (rb, "rb"), (ridx, "ridx"),
                   (sw13, "sw13"), (sw2, "sw2"), (ew1, "ew1"), (ew2, "ew2")]
        NPRJ = 6
        block = ctx.enter_context(nc.Block())

        @block.sync
        def _(sp):
            for dst, name in WEIGHTS:
                sp.dma_start(dst[:], t[name]).then_inc(weights, 16)
            sp.sem_inc(stored, 16)
            with sp.Fori(0, B) as b:
                sp.wait_ge(res_ready, b + 1)
                sp.dma_start(out[:, b, :], res[:]).then_inc(stored, 16)
            sp.wait_ge(weights, 16 * len(WEIGHTS))
            sp.wait_ge(stored, 16 * (B + 1))

        @block.tensor
        def _(pe):
            pe.wait_ge(weights, 16 * len(WEIGHTS))

            def layernorm(b, k):
                pe.wait_ge(ln_in, 2 * b + k + 1)
                pe.matmul(PS[:, 0, :], onesm[:], XR[:, b, :], start=True, stop=True).then_inc(ln_mean, 1)
                pe.wait_ge(ln_sq, 2 * b + k + 1)
                pe.matmul(PS[:, 1, :], onesm[:], lnsq[:], start=True, stop=True).then_inc(ln_var, 1)

            with pe.Fori(0, B) as b:
                layernorm(b, 0)
                pe.wait_ge(h_ready, 2 * b + 1)
                for m in range(2):
                    pe.matmul(PS[:, 2 + m, :], aq[:, m * P:(m + 1) * P], hT[:], start=True, stop=True).then_inc(prj_mm, 1)
                pe.matmul(PS[0:AR, 4, :], akd[:], hT[:], start=True, stop=True).then_inc(prj_mm, 1)
                pe.wait_ge(prj_out, NPRJ * b + 3)
                for m in range(2):
                    pe.matmul(PS[:, 5 + m, :], akv[:, 0, m * P:(m + 1) * P], lat[:], start=True, stop=True).then_inc(prj_mm, 1)
                for i in range(NT):
                    mm = pe.matmul(PS[:, i // 2, (i % 2) * AH * AD:(i % 2 + 1) * AH * AD], lat[:, i * P:(i + 1) * P],
                                   akv[:, 1, :], start=True, stop=True)
                mm.then_inc(prj_mm, 1)
                pe.wait_ge(prj_out, NPRJ * b + NPRJ)

                def score(p):
                    if p >= 2:
                        pe.wait_ge(prob_ready, 2 * NP * b + 2 * (p - 1))
                    i, hp = p // PAIR, p % PAIR
                    for q in range(2):
                        h = 2 * hp + q
                        r = AD * (h % 4)
                        mm = pe.matmul(PS[:, 2 * (p % 2) + q, :], qT[r:r + AD, h // 4, i * P:(i + 1) * P],
                                       kT[r:r + AD, h // 4, :], start=True, stop=True, tile_position=(r, 0))
                    mm.then_inc(sc_mm, 1)

                def prob_T(u):
                    pe.wait_ge(prob_ready, 2 * NP * b + u + 1)
                    if u >= 2:
                        pe.wait_ge(pt_out[u % 2], NP * b + u // 2)
                    for k in range(NT):
                        mm = pe.transpose(PS[:, 4 + u % 2, k * P:(k + 1) * P], prob[:, u % 4, k * P:(k + 1) * P], ident[:])
                    mm.then_inc(pt_tr, 1)

                def times_v(u):
                    i, h = u // AH, u % AH
                    pe.wait_ge(pt_out[u % 2], NP * b + u // 2 + 1)
                    if h == 0 and i >= 2:
                        pe.wait_ge(on_ready, NT * b + i - 1)
                    for k in range(NT):
                        mm = pe.matmul(PS[:, 6 + i % 2, h * AD:(h + 1) * AD], probT[:, u % 2, k, :],
                                       vt[:, k, h * AD:(h + 1) * AD], start=(k == 0), stop=(k == NT - 1))
                    mm.then_inc(o_mm, 1)

                score(0)
                for p in range(NP):
                    if p + 1 < NP:
                        score(p + 1)
                    for q in range(2):
                        u = 2 * p + q
                        prob_T(u)
                        if u:
                            times_v(u - 1)
                times_v(2 * NP - 1)
                pe.wait_ge(on_ready, NT * b + NT)
                for m in range(2):
                    for i in range(NT):
                        mm = pe.transpose(PS[:, 2 + m, i * P:(i + 1) * P], aon[:, i, m * P:(m + 1) * P], ident[:])
                    mm.then_inc(ot_tr, 1)
                for m in range(2):
                    pe.wait_ge(ot_out, 2 * b + m + 1)
                    mm = pe.matmul(PS[:, 0, :], awo[:, m, :], aoT[:, m, :], start=(m == 0), stop=(m == 1))
                mm.then_inc(ay_mm, 1)

                layernorm(b, 1)
                pe.wait_ge(h_ready, 2 * b + 2)
                for i in range(NT):
                    mm = pe.matmul(PS[:, 2, i * NE:(i + 1) * NE], hT[:, i * P:(i + 1) * P], rw[:], start=True, stop=True)
                mm.then_inc(rt_mm, 1)
                for k in range(2):
                    for m in range(2):
                        pe.matmul(PS[:, 4 + 2 * k + m, :], sw13[:, k, m * P:(m + 1) * P], hT[:],
                                  start=True, stop=True).then_inc(sh_mm, 1)
                pe.wait_ge(sh_ready, 2 * b + 2)
                for m in range(2):
                    pe.matmul(PS[:, 0, :], sw2[:, m, :], shg[:, m, :], start=(m == 0), stop=False)
                pe.wait_ge(comb_ready, b + 1)
                for i in range(NT):
                    mm = pe.transpose(PS[0:NE, 3, i * P:(i + 1) * P], comb[:, i, :], ident[:])
                mm.then_inc(ct_tr, 1)
                pe.wait_ge(ct_out, b + 1)

                def hidden(e):
                    if e >= 2:
                        pe.wait_ge(eh_ready, NE * b + e - 1)
                    pe.matmul(PS[:, 4 + e % 2, :], ew1[:, e, :], hT[:], start=True, stop=True).then_inc(eh_mm, 1)
                    if e >= 2:
                        pe.wait_ge(eg_ready, NE * b + e - 1)
                    pe.matmul(PS[:, 6 + e % 2, :], sel8[:, e, :], combT[:], start=True, stop=True).then_inc(cb_mm, 1)

                hidden(0)
                for e in range(NE):
                    if e + 1 < NE:
                        hidden(e + 1)
                    pe.wait_ge(eg_ready, NE * b + e + 1)
                    pe.matmul(PS[:, 0, :], ew2[:, e, :], eg[:, e % 2, :], start=False, stop=(e == NE - 1)).then_inc(ey_mm, 1)

        @block.scalar
        def _(act):
            act.wait_ge(weights, 16 * len(WEIGHTS))

            def layernorm(b, k):
                act.wait_ge(ln_cent, 2 * b + k + 1)
                act.activation(lnsq[:], lnc[:], ACT.Square).then_inc(ln_sq, 1)
                act.wait_ge(ln_var, 2 * b + k + 1)
                act.activation(lnv[:], PS[:, 1, :], ACT.Ln, bias=epsc[:, 0:1]).then_inc(ln_lv, 1)
                act.wait_ge(ln_lv, 2 * b + k + 1)
                act.activation(lnr[:], lnv[:], ACT.Exp, scale=-0.5).then_inc(ln_rstd, 1)

            with act.Fori(0, B) as b:
                layernorm(b, 0)
                prj = [(qT[:, 0, :], PS[:, 2, :]), (qT[:, 1, :], PS[:, 3, :]), (lat[:], PS[0:AR, 4, :]),
                       (kT[:, 0, :], PS[:, 5, :]), (kT[:, 1, :], PS[:, 6, :]),
                       (vt[:].rearrange("p i n -> p (i n)"), PS[:, 0:2, :].rearrange("p a n -> p (a n)"))]
                for n, (dst, src) in enumerate(prj):
                    act.wait_ge(prj_mm, NPRJ * b + n + 1)
                    act.activation(dst, src, ACT.Copy).then_inc(prj_out, 1)

                def probs_out(u):
                    if u % 2:
                        act.wait_ge(pt_tr, 2 * NP * b + u + 1)
                        act.activation(probT[:, 1].rearrange("p a n -> p (a n)"), PS[:, 5, :], ACT.Copy).then_inc(pt_out[1], 1)

                for u in range(2 * NP):
                    p, q = u // 2, u % 2
                    i, h = u // AH, u % AH
                    if q == 0:
                        act.wait_ge(max_ready, NP * b + p + 1)
                    if u >= 4:
                        act.wait_ge(pt_tr, 2 * NP * b + u - 3)
                    act.activation(prob[:, u % 4, :], PS[:, 2 * (p % 2) + q, :], ACT.Exp, bias=anm[:, p % 2, q:q + 1],
                                   scale=SM_SCALE, accum_out=asum[:, i, h:h + 1]).then_inc(prob_ready, 1)
                    if u >= 2:
                        probs_out(u - 2)
                probs_out(2 * NP - 1)
                layernorm(b, 1)
                act.wait_ge(rt_mm, b + 1)
                act.activation(rsg[:].rearrange("p i e -> p (i e)"), PS[:, 2, 0:NT * NE], ACT.Sigmoid).then_inc(sig_ready, 1)
                for m in range(2):
                    act.wait_ge(sh_mm, 4 * b + m + 1)
                    act.activation(shs[:, m, :], PS[:, 4 + m, :], ACT.Silu).then_inc(sh_silu, 1)
                for e in range(NE):
                    act.wait_ge(eh_mm, NE * b + e + 1)
                    if e >= 2:
                        act.wait_ge(eg_ready, NE * b + e - 1)
                    act.activation(eh[:, e % 2, :], PS[:, 4 + e % 2, :], ACT.Gelu).then_inc(eh_ready, 1)

        @block.gpsimd
        def _(pool):
            pool.wait_ge(weights, 16 * len(WEIGHTS))

        @block.vector
        def _(v):
            st = Steps(v, dve_steps)
            v.wait_ge(weights, 16 * len(WEIGHTS))

            def link(ins):
                st.did(ins)
                st.wait()

            def layernorm(b, k, scale, shift):
                v.wait_ge(ln_mean, b * 2 + k + 1)
                v.tensor_tensor(lnc[:], XR[:, b, :], PS[:, 0, :], ALU.subtract).then_inc(ln_cent, 1)
                v.wait_ge(ln_rstd, b * 2 + k + 1)
                v.wait_ge(ln_cent, b * 2 + k + 1)
                link(v.tensor_tensor(lnt[:], lnc[:], lnr[:], ALU.mult))
                v.tensor_scalar(hT[:], lnt[:], scale, shift, ALU.mult, ALU.add).then_inc(h_ready, 1)

            PER = 24
            with v.Fori(0, B) as b:
                st.enter(b, PER)
                v.scalar_tensor_tensor(XR[:, b, :], X[:, b, PADX:PADX + L], mod[:, 0, 5, bass.ds(b, 1)], XR[:, b, :],
                                       ALU.mult, ALU.add).then_inc(ln_in, 1)
                v.wait_ge(ln_in, 2 * b + 1)
                layernorm(b, 0, mod[:, 1, 1, bass.ds(b, 1)], mod[:, 1, 0, bass.ds(b, 1)])

                def row_max(p):
                    v.wait_ge(sc_mm, NP * b + p + 1)
                    v.tensor_reduce(amx[:, p % 2, :], PS[:, 2 * (p % 2):2 * (p % 2) + 2, :], AX.X, ALU.max).then_inc(max_in, 1)
                    v.wait_ge(max_in, NP * b + p + 1)
                    if p >= 2:
                        v.wait_ge(prob_ready, 2 * NP * b + 2 * (p - 1))
                    v.tensor_scalar(anm[:, p % 2, :], amx[:, p % 2, :], -SM_SCALE, None, ALU.mult).then_inc(max_ready, 1)

                def heads_out(i):
                    v.wait_ge(prob_ready, 2 * NP * b + AH * (i + 1))
                    v.reciprocal(arz[:, i, :], asum[:, i, :]).then_inc(rz_ready, 1)
                    v.wait_ge(rz_ready, NT * b + i + 1)
                    v.wait_ge(o_mm, 2 * NP * b + AH * (i + 1))
                    v.tensor_tensor(aon[:, i, :].rearrange("p (h d) -> p h d", h=AH),
                                    PS[:, 6 + i % 2, 0:AH * AD].rearrange("p (h d) -> p h d", h=AH),
                                    arz[:, i, :].unsqueeze(2).to_broadcast([P, AH, AD]), ALU.mult).then_inc(on_ready, 1)

                row_max(0)
                for p in range(NP):
                    if p + 1 < NP:
                        row_max(p + 1)
                    v.wait_ge(pt_tr, 2 * NP * b + 2 * p + 1)
                    v.tensor_copy(probT[:, 0].rearrange("p a n -> p (a n)"), PS[:, 4, :]).then_inc(pt_out[0], 1)
                    if p % PAIR == 0 and p:
                        heads_out(p // PAIR - 1)
                heads_out(NT - 1)
                for m in range(2):
                    v.wait_ge(ot_tr, 2 * b + m + 1)
                    v.tensor_copy(aoT[:, m, :], PS[:, 2 + m, :]).then_inc(ot_out, 1)
                v.wait_ge(ay_mm, b + 1)
                v.scalar_tensor_tensor(XR[:, b, :], PS[:, 0, :], mod[:, 1, 2, bass.ds(b, 1)], XR[:, b, :],
                                       ALU.mult, ALU.add).then_inc(ln_in, 1)
                v.wait_ge(ln_in, 2 * b + 2)
                layernorm(b, 1, mod[:, 1, 4, bass.ds(b, 1)], mod[:, 1, 3, bass.ds(b, 1)])

                v.wait_ge(sig_ready, b + 1)
                wide = lambda x: x.unsqueeze(2).to_broadcast([P, NT, NE])
                every = lambda x: x.unsqueeze(1).to_broadcast([P, NT, NE])
                link(v.tensor_tensor(rt[:, 0], rsg[:], every(rb[:]), ALU.add))
                for k in range(2):
                    sel, eq, idx, hot = rt[:, 4 * k], rt[:, 4 * k + 1], rt[:, 4 * k + 2], rt[:, 4 * k + 3]
                    link(v.tensor_reduce(rm[:, 2 * k, :], sel, AX.X, ALU.max))
                    link(v.tensor_tensor(eq, sel, wide(rm[:, 2 * k, :]), ALU.is_equal))
                    link(v.tensor_tensor(idx, eq, every(ridx[:]), ALU.mult))
                    link(v.tensor_reduce(rm[:, 2 * k + 1, :], idx, AX.X, ALU.max))
                    link(v.tensor_tensor(hot, idx, wide(rm[:, 2 * k + 1, :]), ALU.is_equal))
                    if k == 0:
                        link(v.scalar_tensor_tensor(rt[:, 4], hot, MASKED, sel, ALU.mult, ALU.add))
                link(v.tensor_tensor(rt[:, 8], rt[:, 3], rt[:, 7], ALU.add))
                link(v.tensor_tensor(rt[:, 9], rt[:, 8], rsg[:], ALU.mult))
                link(v.tensor_reduce(rm[:, 4, :], rt[:, 9], AX.X, ALU.add))
                link(v.tensor_scalar(rm[:, 5, :], rm[:, 4, :], DENOM_MIN, None, ALU.add))
                link(v.reciprocal(rm[:, 6, :], rm[:, 5, :]))
                link(v.tensor_scalar(rm[:, 7, :], rm[:, 4, :], DENOM_MIN, None, ALU.is_gt))
                link(v.tensor_tensor(rm[:, 8, :], rm[:, 6, :], rm[:, 7, :], ALU.mult))
                link(v.tensor_scalar(rm[:, 9, :], rm[:, 7, :], -0.5, 0.5, ALU.mult, ALU.add))
                link(v.tensor_tensor(rt[:, 1], rt[:, 9], wide(rm[:, 8, :]), ALU.mult))
                link(v.tensor_tensor(rt[:, 2], rt[:, 8], wide(rm[:, 9, :]), ALU.mult))
                v.tensor_tensor(comb[:], rt[:, 1], rt[:, 2], ALU.add).then_inc(comb_ready, 1)
                for m in range(2):
                    v.wait_ge(sh_silu, 2 * b + m + 1)
                    v.wait_ge(sh_mm, 4 * b + m + 3)
                    v.tensor_tensor(shg[:, m, :], shs[:, m, :], PS[:, 6 + m, :], ALU.mult).then_inc(sh_ready, 1)
                v.wait_ge(ct_tr, b + 1)
                v.tensor_copy(combT[:], PS[0:NE, 3, :]).then_inc(ct_out, 1)
                for e in range(NE):
                    v.wait_ge(eh_ready, NE * b + e + 1)
                    v.wait_ge(cb_mm, NE * b + e + 1)
                    if e >= 2:
                        v.wait_ge(ey_mm, NE * b + e - 1)
                    v.tensor_tensor(eg[:, e % 2, :], eh[:, e % 2, :], PS[:, 6 + e % 2, :], ALU.mult).then_inc(eg_ready, 1)
                v.wait_ge(ey_mm, NE * b + NE)
                v.wait_ge(stored, 16 * (b + 1))
                v.scalar_tensor_tensor(res[:], PS[:, 0, :], mod[:, 1, 5, bass.ds(b, 1)], XR[:, b, :],
                                       ALU.mult, ALU.add).then_inc(res_ready, 1)
                st.leave(B, PER)
            v.wait_ge(res_ready, B)


def build(nc, t, out):
    with ExitStack() as ctx:
        def sb(name, shape):
            return ctx.enter_context(nc.sbuf_tensor(name, shape, F32))

        PS = ctx.enter_context(nc.psum_tensor("PS", [P, 8, 512], F32))
        XR = sb("XR", [P, B, L])
        X = sb("X", [P, B, PADX + L])
        XA = sb("XA", [P, B, 1 + L])
        mod = sb("mod", [P, 2, 6, B])
        onesm = sb("onesm", [P, P])
        ident = sb("ident", [P, P])
        epsc = sb("epsc", [P, 2])
        sel8 = sb("sel8", [8, 8, P])
        mixer(nc, t, XR, X, XA, mod, PS, onesm, ident, epsc, sel8)
        local_layers(nc, t, X, XA, PS, onesm, ident, epsc)
        attention_and_experts(nc, t, XR, X, mod, PS, onesm, ident, epsc, sel8, out)


def rows(w, k=P):
    return w.reshape(-1, k, w.shape[-1]).transpose(1, 0, 2)


def layout(a):
    f = np.float32
    h = {}
    h["xT"] = a["L0_attn_input_tensor"].reshape(B * L, D).T.reshape(D, B, L)
    h["cT"] = np.stack([a["L0_c"].T, a["L1_c"].T], 1)
    h["wmod"] = np.stack([a["L0_wmod"], a["L1_wmod"]], 1)
    h["wxz"] = np.stack([a["L0_attn_Wx"].T, a["L0_attn_Wz"].T], 1)
    conv = np.concatenate([a["L0_attn_conv_w"][:, 0, :], a["L0_attn_conv_b"][:, None]], 1)
    h["convp"] = rows(conv)
    h["wbc"] = np.stack([rows(a["L0_attn_Wb"].T), rows(a["L0_attn_Wc"].T)], 1)
    h["wdt"] = rows(a["L0_attn_Wdt"].T)
    h["head8"] = np.stack([a["L0_attn_b_dt"], a["L0_attn_log_a"]], 1)
    h["featp"] = rows(np.stack([np.repeat(a["L0_attn_d_param"], SP), a["L0_attn_gn_w"], a["L0_attn_gn_b"]], 1))
    h["wout"] = rows(a["L0_attn_Wout"].T)
    wqkv = a["L0_ffn_Wqkv"].reshape(DEPTH, D, 3, NG, GW).transpose(0, 1, 3, 2, 4)
    h["wqkv"] = wqkv.reshape(DEPTH, D, NG, 3 * GW)
    qk = np.stack([a["L0_ffn_q_scale"], a["L0_ffn_k_scale"]], 1)
    swapped = np.concatenate([qk[..., QD // 2:], qk[..., :QD // 2]], -1)
    h["qkg"] = np.broadcast_to(np.stack([qk, swapped], 1)[:, None], (DEPTH, P, 2, 2, QD))
    h["wo"] = a["L0_ffn_Wo"].reshape(DEPTH, NG, 2, P, D).transpose(0, 1, 3, 2, 4)
    h["w1"] = a["L0_ffn_W1"]
    w2 = np.zeros((DEPTH, FK * P, D), f)
    w2[:, :FF] = a["L0_ffn_W2"]
    h["w2"] = w2.reshape(DEPTH, FK, P, D).transpose(0, 2, 1, 3)
    ffp = np.zeros((DEPTH, P, 2 * FK + 3), f)
    for k in range(2):
        b1 = np.zeros((DEPTH, FK * P), f)
        b1[:, :FF] = a["L0_ffn_b1"][:, k * FF:(k + 1) * FF]
        ffp[:, :, k * FK:(k + 1) * FK] = b1.reshape(DEPTH, FK, P).transpose(0, 2, 1)
    ffp[:, :, 2 * FK] = a["L0_ffn_b2"]
    ffp[:, :, 2 * FK + 1] = a["L0_ffn_ln_g"]
    ffp[:, :, 2 * FK + 2] = a["L0_ffn_ln_b"]
    h["ffp"] = ffp
    h["aq"] = a["L1_attn_Wq"].T
    h["akd"] = a["L1_attn_Wkv_down"].T
    h["akv"] = np.stack([a["L1_attn_Wk_up"].T, a["L1_attn_Wv_up"].T], 1)
    h["awo"] = rows(a["L1_attn_Wo"].T)
    h["rw"] = a["L1_ffn_router_w"].T
    h["rb"] = np.broadcast_to(a["L1_ffn_router_bias"], (P, NE))
    h["sw13"] = np.stack([a["L1_ffn_sw1"], a["L1_ffn_sw3"]], 1)
    h["sw2"] = rows(a["L1_ffn_sw2"])
    h["ew1"] = a["L1_ffn_ew1"].transpose(1, 0, 2)
    h["ew2"] = a["L1_ffn_ew2"].transpose(1, 0, 2)
    h["onesm"] = np.full((P, P), 1.0 / D, f)
    h["ident"] = np.eye(P, dtype=f)
    h["sel8"] = np.repeat(np.eye(8, dtype=f)[:, :, None], P, 2)
    h["tri"] = np.triu(np.ones((P, P), f))
    h["grpm"] = np.kron(np.eye(P // SP), np.full((SP, SP), 1.0 / SP)).astype(f)
    h["ridx"] = np.broadcast_to(np.arange(NE, 0, -1).astype(f), (P, NE))
    i = np.arange(P)[:, None] % WIN
    j = np.arange(2 * WIN)[None, :] - WIN
    off = (i < j) | (i > j + WIN)
    first = off | ((j < 0) & (np.arange(P)[:, None] < WIN))
    h["amask"] = np.tile(np.where(np.stack([first, off], 1), f(MASKED), f(0)), (1, 1, GH))
    half = np.arange(0, QD, 2, dtype=f)
    inv = f(1) / np.power(f(10000), half / f(QD), dtype=f)
    fr = (np.arange(L, dtype=f)[:, None] * inv[None]).astype(f).astype(np.float64)
    base = ((half + f(0.4 * QD)) / f(1.4 * QD)).astype(np.float64)
    power = (np.arange(L) - L // 2) / (WIN // 2)
    scale = base[None, :] ** power[:, None]
    two = lambda x, y: np.concatenate([x, y], -1)
    rotc = np.stack([two(np.cos(fr) * scale, np.cos(fr) * scale), two(np.cos(fr) / scale, np.cos(fr) / scale)], 1)
    rots = np.stack([two(-np.sin(fr) * scale, np.sin(fr) * scale), two(-np.sin(fr) / scale, np.sin(fr) / scale)], 1)
    h["rotc"] = rotc.reshape(NT, P, 2, QD).transpose(1, 0, 2, 3)
    h["rots"] = rots.reshape(NT, P, 2, QD).transpose(1, 0, 2, 3)
    return {"in_" + k: np.ascontiguousarray(v, dtype=f) for k, v in h.items()}


def kernel(**inputs):
    import concourse.bacc as bacc
    from concourse.bass_utils import run_bass_kernel_spmd

    nc = bacc.Bacc("TRN2", target_bir_lowering=False, num_devices=1)
    arrays = layout({k: np.asarray(v) for k, v in inputs.items()})
    t = {k[3:]: nc.dram_tensor(k, v.shape, F32, kind="ExternalInput").ap() for k, v in arrays.items()}
    out = nc.dram_tensor("out", (D, B, L), F32, kind="ExternalOutput").ap()
    build(nc, t, out)
    r = run_bass_kernel_spmd(nc, [arrays], core_ids=[0])
    return np.ascontiguousarray(r.results[0]["out"].reshape(D, B * L).T.reshape(B, L, D))
```

```python
from contextlib import ExitStack

import numpy as np
import concourse.bass as bass
from concourse import mybir

F32 = mybir.dt.float32
ALU = mybir.AluOpType
ACT = mybir.ActivationFunctionType
AX = mybir.AxisListType

B, L, D = 4, 512, 128
P = 128
NT = L // P
EPS = 1e-5
GATE_MIN = 0.25
SH, SN, SP = 8, 64, 32
INNER = SH * SP
FM = INNER // P
TAPS = 4
PAIRS = SH // 2
STEPS_A = PAIRS * NT
DEPTH, QH, QD, WIN = 6, 16, 64, 32
GH = 4
NG = QH // GH
GW = GH * QD
NW = P // WIN
UNITS = NG * B * NT
PASSES = NG * B
QK_SCALE = 8.0
NORM_MIN = 1e-12
PADX = WIN + 1
FF = 341
FR = [P, P, FF - 2 * P]
FK = len(FR)
MASKED = -1.0e30
AH, AD, AR = 8, 32, 64
NE = 8
SM_SCALE = AD ** -0.5
DENOM_MIN = 1e-9


EXP_LN_SET = 6


def exp_ln_table(nc):
    nc.scalar.add_instruction(mybir.InstLoadActFuncSet(act_func_set_id=EXP_LN_SET,
                                                       name=nc.get_next_instruction_name()))


class Steps:

    def __init__(self, eng, sem):
        self.eng, self.sem, self.base, self.n, self.held = eng, sem, 0, 0, []

    def did(self, ins):
        ins.then_inc(self.sem, 1)
        self.n += 1
        return self.n

    def wait(self, at=None):
        self.eng.wait_ge(self.sem, self.base + (self.n if at is None else at))

    def enter(self, i, per):
        self.held.append((self.base, self.n))
        self.base, self.n = self.base + self.n + i * per, 0

    def leave(self, trips, per):
        assert self.n == per, f"{self.n} steps in a pass, not {per}"
        self.base, self.n = self.held.pop()
        self.n += trips * per


def mixer(nc, t, XR, X, XA, mod, PS, onesm, ident, epsc, sel8):
    with ExitStack() as ctx:
        def sb(name, shape):
            return ctx.enter_context(nc.sbuf_tensor(name, shape, F32))

        def sem(name):
            return ctx.enter_context(nc.semaphore(name))

        grpm = sb("grpm", [P, P])
        tri = sb("tri", [P, P])
        cT = sb("cT", [P, 2, B])
        wmod = sb("wmod", [P, 2, 6 * D])
        wxz = sb("wxz", [P, 2, INNER])
        convp = sb("convp", [P, FM, TAPS + 1])
        wbc = sb("wbc", [P, 2, FM, SH * SN])
        wdt = sb("wdt", [P, FM, SH])
        head8 = sb("head8", [SH, 2])
        featp = sb("featp", [P, FM, 3])
        wout = sb("wout", [P, FM, D])
        sc = sb("sc", [P, 2, B])
        gtmp = sb("gtmp", [P, 4, 4, B])
        lnc = sb("lnc", [P, 2, L])
        lnsq = sb("lnsq", [P, 2, L])
        lnv = sb("lnv", [P, 2, L])
        lnr = sb("lnr", [P, 2, L])
        lnt = sb("lnt", [P, 2, L])
        hT = sb("hT", [P, L])
        xpad = sb("xpad", [P, FM, TAPS - 1 + L])
        cacc = sb("cacc", [P, FM, TAPS, L])
        xc = sb("xc", [P, FM, L])
        zs = sb("zs", [P, FM, L])
        d8 = sb("d8", [SH, 6, L])
        zero8 = sb("zero8", [SH, L])
        neg_a = sb("neg_a", [SH, 2])
        cols = sb("cols", [P, 2, NT, SH])
        xdt = sb("xdt", [P, NT, INNER])
        bz = sb("bz", [P, 2, PAIRS, L])
        cpair = sb("cpair", [P, PAIRS, L])
        acum = sb("acum", [P, L])
        dec = sb("dec", [P, 2, 2, L])
        wgt = sb("wgt", [P, 2, 2, L])
        ysb = sb("ysb", [P, FM, L])
        bst = sb("bst", [P, FM, 6])
        gst = sb("gst", [P, 2, FM])
        gsm = sb("gsm", [P, 2, FM])
        gv = sb("gv", [P, 8, FM])
        mhalf = sb("mhalf", [P, FM])
        yn = sb("yn", [P, FM, L])
        onorm = sb("onorm", [P, FM, L])

        landed = sem("a_landed")
        weights = sem("a_weights")
        zeroed = sem("a_zeroed")
        mod_mm = sem("mod_mm")
        mod_ready = sem("mod_ready")
        dve_steps = sem("a_dve_steps")
        act_steps = sem("a_act_steps")
        ln_in = sem("a_ln_in")
        ln_mean = [sem(f"a_ln_mean{k}") for k in range(2)]
        ln_cent = [sem(f"a_ln_cent{k}") for k in range(2)]
        ln_sq = [sem(f"a_ln_sq{k}") for k in range(2)]
        ln_var = [sem(f"a_ln_var{k}") for k in range(2)]
        ln_rstd = [sem(f"a_ln_rstd{k}") for k in range(2)]
        h_ready = [sem(f"a_h_ready{k}") for k in range(2)]
        a_done = sem("a_done")
        xz_mm = sem("xz_mm")
        xpad_ready = sem("xpad_ready")
        conv_ready = sem("conv_ready")
        xc_ready = sem("xc_ready")
        zs_ready = sem("zs_ready")
        dt_mm = sem("dt_mm")
        dt_na = sem("dt_na")
        dt_ln = sem("dt_ln")
        acum_ready = sem("acum_ready")
        col_tr = sem("col_tr")
        xtok_tr = sem("xtok_tr")
        xdt_ready = sem("xdt_ready")
        bc_mm = sem("bc_mm")
        bc_ready = sem("bc_ready")
        ab_mm = sem("ab_mm")
        g_mm = sem("g_mm")
        dec_in = sem("dec_in")
        dec_exp = sem("dec_exp")
        dec_tri = sem("dec_tri")
        w_ready = sem("w_ready")
        y_mm = sem("y_mm")
        gs_in = sem("gs_in")
        gs_mm = sem("gs_mm")
        gv_ready = sem("gv_ready")
        gr_ready = sem("gr_ready")
        on_ready = sem("on_ready")
        wout_mm = sem("wout_mm")

        FIRST = [(cT, "cT"), (wmod, "wmod"), (XR, "xT"), (onesm, "onesm"), (ident, "ident")]
        REST = [(wxz, "wxz"), (convp, "convp"), (wdt, "wdt"), (head8, "head8"), (featp, "featp"),
                (wbc, "wbc"), (sel8, "sel8"), (tri, "tri"), (grpm, "grpm"), (wout, "wout")]
        LNB = ((4, 5), (0, 1))
        block = ctx.enter_context(nc.Block())

        @block.sync
        def _(sp):
            for dst, name in FIRST:
                sp.dma_start(dst[:], t[name]).then_inc(landed, 16)
            for dst, name in REST:
                sp.dma_start(dst[:], t[name]).then_inc(weights, 16)
            sp.wait_ge(landed, 16 * len(FIRST))
            sp.wait_ge(weights, 16 * len(REST))

        @block.tensor
        def _(pe):
            mm = None
            pe.wait_ge(landed, 16 * len(FIRST))
            pe.wait_ge(act_steps, 1)
            for blk in range(2):
                for k in range(6):
                    n = (blk * 6 + k) * B
                    mm = pe.matmul(PS[:, 7, n:n + B], wmod[:, blk, k * D:(k + 1) * D], sc[:, blk, :],
                                   start=True, stop=True)
            mm.then_inc(mod_mm, 1)
            pe.wait_ge(mod_ready, 1)
            pe.wait_ge(weights, 16 * len(REST))

            def mean(b, k):
                pe.matmul(PS[:, LNB[k][0], :], onesm[:], XR[:, b % B, :], start=True, stop=True).then_inc(ln_mean[k], 1)

            def var(b, k):
                pe.wait_ge(ln_sq[k], b + 1)
                pe.matmul(PS[:, LNB[k][1], :], onesm[:], lnsq[:, k, :], start=True, stop=True).then_inc(ln_var[k], 1)

            def project(b):
                pe.wait_ge(h_ready[0], b + 1)
                for k in range(2):
                    for m in range(FM):
                        pe.matmul(PS[:, 2 + 2 * k + m, :], wxz[:, k, m * P:(m + 1) * P], hT[:],
                                  start=True, stop=True).then_inc(xz_mm, 1)

            mean(0, 0)
            var(0, 0)
            project(0)
            with pe.Fori(0, B) as b:
                pe.wait_ge(a_done, b + 1)
                pe.wait_ge(xc_ready, FM * b + FM)
                for m in range(FM):
                    mm = pe.matmul(PS[0:SH, 6, :], wdt[:, m, :], xc[:, m, :], start=(m == 0), stop=(m == FM - 1))
                mm.then_inc(dt_mm, 1)
                for i in range(NT):
                    for m in range(FM):
                        mm = pe.transpose(PS[:, i // 2, (i % 2) * INNER + m * P:(i % 2) * INNER + (m + 1) * P],
                                          xc[:, m, i * P:(i + 1) * P], ident[:])
                mm.then_inc(xtok_tr, 1)
                for n in range(2 * PAIRS):
                    which, m = n // PAIRS, n % PAIRS
                    if n < 2:
                        pe.wait_ge(xpad_ready, FM * b + FM)
                    elif n < 4:
                        pe.wait_ge(zs_ready, FM * b + FM)
                    else:
                        pe.wait_ge(bc_ready, 2 * PAIRS * b + n - 3)
                    for k in range(FM):
                        mm = pe.matmul(PS[:, 2 + n % 4, :], wbc[:, which, k, m * P:(m + 1) * P], xc[:, k, :],
                                       start=(k == 0), stop=(k == FM - 1))
                    mm.then_inc(bc_mm, 1)
                pe.wait_ge(acum_ready, b + 1)
                for q in range(2):
                    for i in range(NT):
                        n = (q * NT + i) * SH
                        src = d8[:, 4, :] if q == 0 else acum[0:SH, :]
                        mm = pe.matmul(PS[:, 6, n:n + SH], src[:, i * P:(i + 1) * P], ident[0:SH, 0:SH],
                                       start=True, stop=True)
                mm.then_inc(col_tr, 1)
                pe.wait_ge(xdt_ready, b + 1)

                def outputs(g):
                    m, i = g // NT, g % NT
                    pe.wait_ge(w_ready, STEPS_A * b + g + 1)
                    for q in range(2):
                        h = 2 * m + q
                        r = SP * (h % 4)
                        mm = pe.matmul(PS[r:r + SP, 6 + h // 4, i * P:L], xdt[:, i, h * SP:(h + 1) * SP],
                                       wgt[:, g % 2, q, 0:L - i * P], start=(i == 0), stop=(i == NT - 1),
                                       tile_position=(0, r))
                    mm.then_inc(y_mm, 1)

                for g in range(STEPS_A):
                    m, i = g // NT, g % NT
                    if i == 0:
                        if m:
                            pe.wait_ge(dec_in, STEPS_A * b + g)
                        for q in range(2):
                            mm = pe.matmul(PS[:, q, :], sel8[:, 2 * m + q, :], acum[:], start=True, stop=True)
                        mm.then_inc(ab_mm, 1)
                    if g < 2:
                        pe.wait_ge(bc_ready, 2 * PAIRS * b + 2 * PAIRS)
                    else:
                        pe.wait_ge(w_ready, STEPS_A * b + g - 1)
                    for q in range(2):
                        mm = pe.matmul(PS[:, 2 + 2 * (g % 2) + q, 0:L - i * P],
                                       bz[:, q, m, i * P:(i + 1) * P], cpair[:, m, i * P:L],
                                       start=True, stop=True)
                    mm.then_inc(g_mm, 1)
                    if g:
                        outputs(g - 1)
                outputs(STEPS_A - 1)
                mean(b + 1, 0)
                pe.wait_ge(gs_in, b + 1)
                pe.matmul(PS[:, 2, 0:2 * FM], grpm[:], gst[:].rearrange("p a b -> p (a b)"),
                          start=True, stop=True).then_inc(gs_mm, 1)
                var(b + 1, 0)
                pe.wait_ge(on_ready, b + 1)
                for m in range(FM):
                    mm = pe.matmul(PS[:, 3, :], wout[:, m, :], onorm[:, m, :], start=(m == 0), stop=(m == FM - 1))
                mm.then_inc(wout_mm, 1)
                pe.wait_ge(ln_in, b + 1)
                mean(b, 1)
                project(b + 1)
                var(b, 1)

        @block.scalar
        def _(act):
            st = Steps(act, act_steps)
            act.wait_ge(landed, 16 * len(FIRST))
            st.did(act.activation(sc[:], cT[:], ACT.Silu))
            act.wait_ge(zeroed, 1)
            act.wait_ge(weights, 16 * len(REST))
            st.did(act.activation(neg_a[:, 0:1], head8[:, 1:2], ACT.Exp))

            def layernorm(b, k):
                act.wait_ge(ln_cent[k], b + 1)
                act.activation(lnsq[:, k, :], lnc[:, k, :], ACT.Square).then_inc(ln_sq[k], 1)
                act.wait_ge(ln_var[k], b + 1)
                st.did(act.activation(lnv[:, k, :], PS[:, LNB[k][1], :], ACT.Ln, bias=epsc[:, 0:1]))
                st.wait()
                act.activation(lnr[:, k, :], lnv[:, k, :], ACT.Exp, scale=-0.5).then_inc(ln_rstd[k], 1)

            PER = 3
            exp_ln_table(nc)
            layernorm(0, 0)
            with act.Fori(0, B) as b:
                st.enter(b, PER)
                for m in range(FM):
                    act.wait_ge(xz_mm, 2 * FM * b + m + 1)
                    act.activation(xpad[:, m, TAPS - 1:TAPS - 1 + L], PS[:, 2 + m, :], ACT.Copy).then_inc(xpad_ready, 1)
                for m in range(FM):
                    act.wait_ge(xz_mm, 2 * FM * b + FM + m + 1)
                    act.activation(zs[:, m, :], PS[:, 4 + m, :], ACT.Silu).then_inc(zs_ready, 1)
                for m in range(FM):
                    act.wait_ge(conv_ready, FM * b + m + 1)
                    act.activation(xc[:, m, :], cacc[:, m, TAPS - 1, :], ACT.Silu,
                                   bias=convp[:, m, TAPS:TAPS + 1]).then_inc(xc_ready, 1)
                exp_ln_table(nc)
                act.wait_ge(dt_na, b + 1)
                st.did(act.activation(d8[:, 2, :], d8[:, 2, :], ACT.Exp))
                st.wait()
                act.activation(d8[:, 3, :], d8[:, 2, :], ACT.Ln, bias=epsc[0:SH, 1:2]).then_inc(dt_ln, 1)
                for n in range(2 * PAIRS):
                    act.wait_ge(bc_mm, 2 * PAIRS * b + n + 1)
                    if n < PAIRS:
                        for q in range(2):
                            r = q * SN
                            ins = act.activation(bz[r:r + SN, q, n, :], PS[r:r + SN, 2 + n % 4, :], ACT.Copy)
                    else:
                        ins = act.activation(cpair[:, n - PAIRS, :], PS[:, 2 + n % 4, :], ACT.Copy)
                    ins.then_inc(bc_ready, 1)
                for g in range(STEPS_A):
                    n = L - (g % NT) * P
                    act.wait_ge(dec_in, STEPS_A * b + g + 1)
                    act.activation(dec[:, g % 2, :, 0:n], dec[:, g % 2, :, 0:n], ACT.Exp).then_inc(dec_exp, 1)
                layernorm(b + 1, 0)
                layernorm(b, 1)
                st.leave(B, PER)

        @block.gpsimd
        def _(pool):
            pool.memset(xpad[:, :, 0:TAPS - 1], 0.0)
            pool.memset(mhalf[:], -0.5)
            pool.memset(zero8[:], 0.0)
            pool.memset(acum[:], 0.0)
            pool.memset(bz[:], 0.0)
            pool.memset(X[:, :, 0:PADX], 0.0)
            pool.memset(epsc[:, 0:1], EPS)
            pool.memset(epsc[:, 1:2], 1.0)
            pool.memset(XA[:, :, 0:1], 0.0).then_inc(zeroed, 1)
            pool.wait_ge(zeroed, 1)
            pool.wait_ge(weights, 16 * len(REST))
            with pool.Fori(0, B) as b:
                for g in range(STEPS_A):
                    pool.wait_ge(dec_exp, STEPS_A * b + g + 1)
                    pool.tensor_tensor(dec[:, g % 2, :, 0:P], dec[:, g % 2, :, 0:P],
                                       tri[:].unsqueeze(1).to_broadcast([P, 2, P]), ALU.mult).then_inc(dec_tri, 1)
                pool.wait_ge(gv_ready, b + 1)
                pool.tensor_tensor(gv[:, 2, :], gv[:, 1, :], mhalf[:], ALU.pow).then_inc(gr_ready, 1)

        @block.vector
        def _(v):
            st = Steps(v, dve_steps)

            def link(ins):
                st.did(ins)
                st.wait()

            v.wait_ge(mod_mm, 1)
            link(v.tensor_copy(mod[:].rearrange("p a k b -> p (a k b)"), PS[:, 7, 0:12 * B]))
            for blk in range(2):
                for k in (1, 4):
                    st.did(v.tensor_scalar(mod[:, blk, k, :], mod[:, blk, k, :], 1.0, None, ALU.add))
                for j, k in enumerate((2, 5)):
                    g = mod[:, blk, k, :]
                    n = blk * 2 + j
                    st.did(v.tensor_scalar(gtmp[:, 0, n, :], g, 0.0, 2.0, ALU.is_ge, ALU.mult))
                    st.did(v.tensor_scalar(gtmp[:, 1, n, :], g, -1.0, None, ALU.mult))
                    st.wait()
                    st.did(v.tensor_tensor(gtmp[:, 2, n, :], gtmp[:, 1, n, :], g, ALU.max))
                    st.wait()
                    st.did(v.tensor_scalar(gtmp[:, 2, n, :], gtmp[:, 2, n, :], GATE_MIN, None, ALU.max))
                    st.did(v.tensor_scalar(gtmp[:, 3, n, :], gtmp[:, 0, n, :], 1.0, None, ALU.subtract))
                    st.wait()
                    st.did(v.tensor_tensor(g, gtmp[:, 3, n, :], gtmp[:, 2, n, :], ALU.mult))
            st.wait()
            v.wait_ge(weights, 16 * len(REST))
            v.wait_ge(zeroed, 1)
            v.wait_ge(act_steps, 2)
            v.tensor_scalar(neg_a[:, 1:2], neg_a[:, 0:1], -1.0, None, ALU.mult).then_inc(mod_ready, 1)
            v.wait_ge(mod_ready, 1)
            v.sem_inc(a_done)

            def centre(b, k):
                v.wait_ge(ln_mean[k], b + 1)
                v.tensor_tensor(lnc[:, k, :], XR[:, b % B, :], PS[:, LNB[k][0], :], ALU.subtract).then_inc(ln_cent[k], 1)

            def normed(b, k, dst):
                v.wait_ge(ln_rstd[k], b + 1)
                v.wait_ge(ln_cent[k], b + 1)
                c, w, r, n = lnc[:, k, :], lnv[:, k, :], lnr[:, k, :], lnt[:, k, :]
                link(v.scalar_tensor_tensor(w, PS[:, LNB[k][1], :], epsc[:, 0:1], r, ALU.add, ALU.mult))
                link(v.scalar_tensor_tensor(n, w, -0.5, r, ALU.mult, ALU.mult))
                link(v.scalar_tensor_tensor(w, n, 1.5, r, ALU.add, ALU.mult))
                link(v.tensor_tensor(n, c, w, ALU.mult))
                v.tensor_scalar(dst, n, mod[:, 0, 3 * k + 1, bass.ds(b % B, 1)], mod[:, 0, 3 * k, bass.ds(b % B, 1)],
                                ALU.mult, ALU.add).then_inc(h_ready[k], 1)

            PER = 38
            centre(0, 0)
            normed(0, 0, hT[:])
            with v.Fori(0, B) as b:
                st.enter(b, PER)
                for m in range(FM):
                    v.wait_ge(xpad_ready, FM * b + m + 1)
                    link(v.tensor_scalar(cacc[:, m, 0, :], xpad[:, m, 0:L], convp[:, m, 0:1], None, ALU.mult))
                    for k in range(1, TAPS):
                        ins = v.scalar_tensor_tensor(cacc[:, m, k, :], xpad[:, m, k:k + L], convp[:, m, k:k + 1],
                                                     cacc[:, m, k - 1, :], ALU.mult, ALU.add)
                        if k < TAPS - 1:
                            link(ins)
                        else:
                            ins.then_inc(conv_ready, 1)
                v.wait_ge(dt_mm, b + 1)
                link(v.tensor_scalar(d8[:, 0, :], PS[0:SH, 6, :], head8[:, 0:1], None, ALU.add))
                link(v.tensor_scalar(d8[:, 1, :], d8[:, 0, :], -1.0, None, ALU.mult))
                v.tensor_tensor(d8[:, 2, :], d8[:, 0, :], d8[:, 1, :], ALU.min).then_inc(dt_na, 1)
                v.wait_ge(dt_ln, b + 1)
                link(v.scalar_tensor_tensor(d8[:, 4, :], d8[:, 0, :], 0.0, d8[:, 3, :], ALU.max, ALU.add))
                link(v.tensor_scalar(d8[:, 5, :], d8[:, 4, :], neg_a[:, 1:2], None, ALU.mult))
                v.tensor_tensor_scan(acum[0:SH, :], d8[:, 5, :], zero8[:], 0.0, ALU.add, ALU.add).then_inc(acum_ready, 1)
                v.wait_ge(col_tr, b + 1)
                link(v.tensor_copy(cols[:].rearrange("p a i h -> p (a i h)"), PS[:, 6, 0:2 * NT * SH]))
                v.wait_ge(xtok_tr, b + 1)
                for k in range(2):
                    ins = v.tensor_tensor(xdt[:, 2 * k:2 * k + 2, :].rearrange("p i (h w) -> p (i h) w", w=SP),
                                          PS[:, k, :].rearrange("p (n w) -> p n w", w=SP),
                                          cols[:, 0, 2 * k:2 * k + 2, :].rearrange("p i h -> p (i h)").unsqueeze(2)
                                          .to_broadcast([P, 2 * SH, SP]), ALU.mult)
                ins.then_inc(xdt_ready, 1)

                def weigh(g):
                    n = L - (g % NT) * P
                    v.wait_ge(dec_tri, STEPS_A * b + g + 1)
                    v.wait_ge(g_mm, STEPS_A * b + g + 1)
                    if g >= 2:
                        v.wait_ge(y_mm, STEPS_A * b + g - 1)
                    k = 2 + 2 * (g % 2)
                    v.tensor_tensor(wgt[:, g % 2, :, 0:n], dec[:, g % 2, :, 0:n], PS[:, k:k + 2, 0:n],
                                    ALU.mult).then_inc(w_ready, 1)

                for g in range(STEPS_A):
                    m, i = g // NT, g % NT
                    if i == 0:
                        v.wait_ge(ab_mm, PAIRS * b + m + 1)
                    if g >= 2:
                        v.wait_ge(w_ready, STEPS_A * b + g - 1)
                    for q in range(2):
                        h = 2 * m + q
                        ins = v.tensor_scalar(dec[:, g % 2, q, 0:L - i * P], PS[:, q, i * P:L],
                                              cols[:, 1, i, h:h + 1], 0.0, ALU.subtract, ALU.min)
                    ins.then_inc(dec_in, 1)
                    if g:
                        weigh(g - 1)
                weigh(STEPS_A - 1)
                centre(b + 1, 0)
                v.wait_ge(y_mm, STEPS_A * b + STEPS_A)
                for m in range(FM):
                    link(v.scalar_tensor_tensor(ysb[:, m, :], xc[:, m, :], featp[:, m, 0:1], PS[:, 6 + m, :],
                                                ALU.mult, ALU.add))
                    link(v.bn_stats(bst[:, m, :], ysb[:, m, :]))
                link(v.tensor_tensor(gv[:, 0, :], bst[:, :, 1], bst[:, :, 4], ALU.add))
                link(v.tensor_scalar(gst[:, 0, :], gv[:, 0, :], 0.5, None, ALU.mult))
                link(v.tensor_tensor(gv[:, 3, :], bst[:, :, 1], bst[:, :, 1], ALU.mult))
                link(v.tensor_tensor(gv[:, 4, :], bst[:, :, 4], bst[:, :, 4], ALU.mult))
                link(v.tensor_tensor(gv[:, 5, :], gv[:, 3, :], gv[:, 4, :], ALU.add))
                link(v.tensor_tensor(gv[:, 6, :], bst[:, :, 2], bst[:, :, 5], ALU.add))
                link(v.tensor_scalar(gv[:, 7, :], gv[:, 6, :], 1.0 / L, None, ALU.mult))
                ins = v.scalar_tensor_tensor(gst[:, 1, :], gv[:, 5, :], 0.5, gv[:, 7, :], ALU.mult, ALU.add)
                ins.then_inc(gs_in, 1)
                v.wait_ge(gs_mm, b + 1)
                link(v.tensor_copy(gsm[:].rearrange("p a b -> p (a b)"), PS[:, 2, 0:2 * FM]))
                link(v.tensor_tensor(gv[:, 0, :], gsm[:, 0, :], gsm[:, 0, :], ALU.mult))
                link(v.tensor_tensor(gv[:, 3, :], gsm[:, 1, :], gv[:, 0, :], ALU.subtract))
                v.tensor_scalar(gv[:, 1, :], gv[:, 3, :], 0.0, EPS, ALU.max, ALU.add).then_inc(gv_ready, 1)
                v.wait_ge(gr_ready, b + 1)
                link(v.tensor_tensor(gv[:, 4, :], gv[:, 2, :], featp[:, :, 1], ALU.mult))
                link(v.tensor_tensor(gv[:, 5, :], gsm[:, 0, :], gv[:, 4, :], ALU.mult))
                link(v.tensor_tensor(gv[:, 6, :], featp[:, :, 2], gv[:, 5, :], ALU.subtract))
                v.wait_ge(zs_ready, FM * b + FM)
                for m in range(FM):
                    link(v.tensor_scalar(yn[:, m, :], ysb[:, m, :], gv[:, 4, m:m + 1], gv[:, 6, m:m + 1],
                                         ALU.mult, ALU.add))
                    ins = v.tensor_tensor(onorm[:, m, :], yn[:, m, :], zs[:, m, :], ALU.mult)
                ins.then_inc(on_ready, 1)
                normed(b + 1, 0, hT[:])
                v.wait_ge(wout_mm, b + 1)
                v.scalar_tensor_tensor(XR[:, b, :], PS[:, 3, :], mod[:, 0, 2, bass.ds(b, 1)], XR[:, b, :],
                                       ALU.mult, ALU.add).then_inc(ln_in, 1)
                v.wait_ge(ln_in, b + 1)
                centre(b, 1)
                normed(b, 1, X[:, b, PADX:PADX + L])
                v.wait_ge(h_ready[1], b + 1)
                v.tensor_copy(XA[:, b, 1:1 + L], X[:, b, PADX:PADX + L]).then_inc(a_done, 1)
                st.leave(B, PER)
            v.wait_ge(a_done, B + 1)


def local_layers(nc, t, X, XA, PS, onesm, ident, epsc):
    with ExitStack() as ctx:
        def sb(name, shape):
            return ctx.enter_context(nc.sbuf_tensor(name, shape, F32))

        def sem(name):
            return ctx.enter_context(nc.semaphore(name))

        HW = QD // 2
        LAST = NT
        BQK, BPV, BV, BRT, BS, BPT = 0, (7, 1), 2, 3, 4, 6
        BO = 4 * 2 * WIN

        amask = sb("amask", [P, 2, GH * 2 * WIN])
        rotc = sb("rotc", [P, NT, 2, QD])
        rots = sb("rots", [P, NT, 2, QD])
        wqkv = sb("wqkv", [P, NG, 3 * GW])
        qkg = sb("qkg", [P, 2, 2, QD])
        wog = sb("wog", [P, 2, D])
        w1 = sb("w1", [P, 2 * FF])
        w2 = sb("w2", [P, FK, D])
        ffp = sb("ffp", [P, 2 * FK + 3])
        xst = sb("xst", [P, NT, P])
        qk = sb("qk", [P, 2, 2, GH, QD])
        qksq = sb("qksq", [P, 2, GH, QD])
        ssr = sb("ssr", [P, 2 * GH])
        ssq = sb("ssq", [P, 2, 2 * GH])
        lnss = sb("lnss", [P, 2 * GH])
        rn = sb("rn", [P, 2, 2 * GH])
        rc = sb("rc", [P, NT, 2, QD])
        rs = sb("rs", [P, NT, 2, QD])
        qkn = sb("qkn", [P, 2, 2, GH, QD])
        qkc = sb("qkc", [P, 2, 2, GH, QD])
        qks = sb("qks", [P, 2, 2, GH, QD])
        qkr = sb("qkr", [P, 2, 2, GH, QD])
        qT = sb("qT", [P, 2, 2, P])
        kT = sb("kT", [P, 2, WIN + L])
        vab = sb("vab", [P, NT, 2, GW])
        sm = sb("sm", [P, GH, 2 * WIN])
        smx = sb("smx", [P, GH])
        smd = sb("smd", [P, 2, GH, 2 * WIN])
        pex = sb("pex", [P, 2, GH, 2 * WIN])
        zsum = sb("zsum", [P, GH])
        zinv = sb("zinv", [P, 2, GH])
        pn = sb("pn", [P, 2, GH, 2, 2 * WIN])
        pT = sb("pT", [P, 2, GH, 2 * WIN])
        oT = sb("oT", [P, 2, L])
        fx = sb("fx", [P, B, L])
        fc = sb("fc", [P, B, L])
        fsq = sb("fsq", [P, B, L])
        flv = sb("flv", [P, B, L])
        frs = sb("frs", [P, B, L])
        fvr = sb("fvr", [P, B, L])
        fvrr = sb("fvrr", [P, B, L])
        fu = sb("fu", [P, B, L])
        fn = sb("fn", [P, B, L])
        fh = sb("fh", [P, B, L])
        fg = sb("fg", [P, FK, L])
        fa = sb("fa", [P, FK, L])

        tables = sem("b_tables")
        zeroed = sem("b_zeroed")
        xst_in = [sem(f"xst_in{i}") for i in range(NT)]
        w_in = sem("w_in")
        wo_in = sem("wo_in")
        ffw_in = sem("ffw_in")
        scaled = sem("scaled")
        qk_mm = sem("qk_mm")
        v_mm = sem("v_mm")
        qk_out = sem("qk_out")
        v_out = sem("v_out")
        v_sh = [sem(f"v_sh{i}") for i in range(NT)]
        sq_sum = sem("sq_sum")
        sq_ready = sem("sq_ready")
        ln_ready = sem("ln_ready")
        rn_ready = sem("rn_ready")
        n_ready = sem("n_ready")
        cos_done = sem("cos_done")
        sin_done = sem("sin_done")
        r_ready = sem("r_ready")
        rt_tr = sem("rt_tr")
        rt_out = sem("rt_out")
        s_mm = sem("s_mm")
        s_out = sem("s_out")
        mx_ready = sem("mx_ready")
        d_ready = sem("d_ready")
        e_ready = sem("e_ready")
        z_ready = sem("z_ready")
        zi_ready = sem("zi_ready")
        p_ready = sem("p_ready")
        p2_ready = sem("p2_ready")
        pt_tr = sem("pt_tr")
        pt_out = sem("pt_out")
        pv_mm = sem("pv_mm")
        pv_out = sem("pv_out")
        wo_mm = sem("wo_mm")
        passed = sem("passed")
        att_done = sem("att_done")
        ff_x = [sem(f"ff_x{b}") for b in range(B)]
        ff_mean = sem("ff_mean")
        ff_c = sem("ff_c")
        ff_sq = sem("ff_sq")
        ff_var = sem("ff_var")
        ff_lv = sem("ff_lv")
        ff_rs = sem("ff_rs")
        ff_vr = sem("ff_vr")
        ff_vrr = sem("ff_vrr")
        ff_u = sem("ff_u")
        ff_n = sem("ff_n")
        ff_h = sem("ff_h")
        ff_gm = sem("ff_gm")
        ff_g = sem("ff_g")
        ff_am = sem("ff_am")
        ff_a = sem("ff_a")
        ff_ym = sem("ff_ym")
        ff_new = sem("ff_new")
        ff_done = sem("ff_done")

        def stage(s, it, lag):
            d = s - lag
            w = it + d // NT
            return d % NT, w, not isinstance(it, int) or 0 <= w < PASSES

        def layers(eng, step, before=None, after=None):
            with eng.Fori(0, DEPTH) as l:
                if before:
                    before(l)
                for s in range(NT):
                    step(l, 0, s)
                with eng.Fori(1, PASSES) as it:
                    for s in range(NT):
                        step(l, it, s)
                for s in range(LAST):
                    step(l, PASSES, s)
                if after:
                    after(l)

        def units(l, w, tile):
            return l * UNITS + w * NT + (tile + 1)

        def first(w, tile, n=1):
            return isinstance(w, int) and w * NT + tile < n

        block = ctx.enter_context(nc.Block())

        @block.sync
        def _(sp):
            for dst, name in ((amask, "amask"), (rotc, "rotc"), (rots, "rots")):
                sp.dma_start(dst[:], t[name]).then_inc(tables, 16)

            def load_x(l, w, tile):
                if not first(w, tile, NT):
                    sp.wait_ge(v_mm, 1 + units(l, w, tile) - NT)
                b = w % B
                lo = tile * P + PADX - 1
                sp.dma_start(xst[0:HALF, tile, :], X[0:HALF, b, lo + 1:lo + 1 + P]).then_inc(xst_in[tile], 16)
                sp.dma_start(xst[HALF:P, tile, :], X[HALF:P, b, lo:lo + P]).then_inc(xst_in[tile], 16)

            def shift_v(l, w, tile):
                if first(w, tile, 3):
                    sp.wait_ge(v_out, units(l, w, tile))
                else:
                    sp.wait_ge(pv_out, units(l, w, tile) - 3)
                sp.dma_start(vab[WIN:P, tile, 1, :], vab[0:P - WIN, tile, 0, :]).then_inc(v_sh[tile], 16)
                if tile + 1 < NT:
                    sp.dma_start(vab[0:WIN, tile + 1, 1, :], vab[P - WIN:P, tile, 0, :]).then_inc(v_sh[tile], 16)

            def load_wo(l, w):
                sp.wait_ge(wo_mm, 1 + l * UNITS + w * NT)
                sp.dma_start(wog[:], t["wo"][l, w // B]).then_inc(wo_in, 16)

            HALF = D // 2
            with sp.Fori(0, DEPTH) as l:
                sp.wait_ge(v_mm, 1 + l * UNITS)
                sp.dma_start(wqkv[:], t["wqkv"][l]).then_inc(w_in, 16)
                sp.wait_ge(scaled, 1 + 2 * l)
                sp.dma_start(qkg[:], t["qkg"][l]).then_inc(w_in, 16)
                sp.wait_ge(ff_done, B * l + 1)
                for tile in range(NT):
                    load_x(l, 0, tile)
                sp.wait_ge(ff_done, B * l + B)
                sp.dma_start(ffp[:], t["ffp"][l]).then_inc(ffw_in, 16)
                load_wo(l, 0)
                for tile in range(NT):
                    load_x(l, 1, tile)
                    shift_v(l, 0, tile)
                sp.dma_start(w1[:], t["w1"][l]).then_inc(ffw_in, 16)
                sp.dma_start(w2[:], t["w2"][l]).then_inc(ffw_in, 16)
                with sp.Fori(1, PASSES - 1) as w:
                    for tile in range(NT):
                        if tile == NT - 1:
                            load_wo(l, w)
                        load_x(l, w + 1, tile)
                        shift_v(l, w, tile)
                for tile in range(NT):
                    if tile == NT - 1:
                        load_wo(l, PASSES - 1)
                    shift_v(l, PASSES - 1, tile)
                for b in range(B):
                    sp.wait_ge(att_done, UNITS * (l + 1) - NT * (B - 1 - b))
                    sp.dma_start(fx[0:HALF, b, :], XA[0:HALF, b, 1:1 + L]).then_inc(ff_x[b], 16)
                    sp.dma_start(fx[HALF:D, b, :], XA[HALF:D, b, 0:L]).then_inc(ff_x[b], 16)
            sp.wait_ge(tables, 48)

        @block.tensor
        def _(pe):
            def rotated_T(l, w, tile):
                pe.wait_ge(r_ready, units(l, w, tile))
                if not first(w, tile):
                    pe.wait_ge(rt_out, units(l, w, tile) - 1)
                for k in range(4):
                    mm = pe.transpose(PS[:, BRT, k * P:(k + 1) * P],
                                      qkr[:, tile % 2, k // 2, (k % 2) * 2:(k % 2) * 2 + 2, :]
                                      .rearrange("p h d -> p (h d)"), ident[:])
                mm.then_inc(rt_tr, 1)

            def project_qk(l, w, tile):
                pe.wait_ge(xst_in[tile], 32 * (l * PASSES + w + 1))
                if not first(w, tile):
                    pe.wait_ge(qk_out, units(l, w, tile) - 1)
                pe.matmul(PS[:, BQK, :], xst[:, tile, :], wqkv[:, w // B, 0:2 * GW],
                          start=True, stop=True).then_inc(qk_mm, 1)

            def project_v(l, w, tile):
                if not first(w, tile):
                    pe.wait_ge(v_out, units(l, w, tile) - 1)
                pe.matmul(PS[:, BV, 0:GW], xst[:, tile, :], wqkv[:, w // B, 2 * GW:3 * GW],
                          start=True, stop=True).then_inc(v_mm, 1)

            def probs_T(l, w, tile):
                pe.wait_ge(p_ready, units(l, w, tile))
                pe.wait_ge(p2_ready, units(l, w, tile))
                if not first(w, tile):
                    pe.wait_ge(pt_out, 2 * units(l, w, tile) - 2)
                for k in range(GH):
                    mm = pe.transpose(PS[:, BPT, k * P:(k + 1) * P],
                                      pn[:, tile % 2, k, :, :].rearrange("p a k -> p (a k)"), ident[:])
                mm.then_inc(pt_tr, 1)

            def scores(l, w, tile):
                pe.wait_ge(rt_out, units(l, w, tile))
                if not first(w, tile, 3):
                    pe.wait_ge(att_done, units(l, w, tile) - 3)
                elif not first(w, tile):
                    pe.wait_ge(s_out, units(l, w, tile) - 1)
                pe.sem_inc(passed)
                for j in range(NW):
                    for e in range(GH):
                        r = QD * (e % 2)
                        mm = pe.matmul(PS[WIN * j:WIN * (j + 1), BS + e % 2, 2 * WIN * (e // 2):2 * WIN * (e // 2 + 1)],
                                       qT[r:r + QD, tile % 2, e // 2, WIN * j:WIN * (j + 1)],
                                       kT[r:r + QD, e // 2, tile * P + WIN * j:tile * P + WIN * (j + 2)],
                                       start=True, stop=True)
                mm.then_inc(s_mm, 1)

            def times_v(l, w, tile):
                pe.wait_ge(pt_out, 2 * units(l, w, tile) - 1)
                for i in range(max(tile - 1, 0), tile + 1):
                    pe.wait_ge(v_sh[i], (16 if i == NT - 1 else 32) * (l * PASSES + w + 1))
                if not first(w, tile):
                    pe.wait_ge(pv_out, units(l, w, tile) - 1)
                pe.sem_inc(passed)
                for half in range(2):
                    if half:
                        pe.wait_ge(pt_out, 2 * units(l, w, tile))
                        pe.sem_inc(passed)
                    for e in range(GH):
                        for jj in range(2):
                            r, o = QD * half, QD * (e % 2)
                            mm = pe.matmul(PS[o:o + QD, BPV[half], (e // 2) * 2 * WIN + jj * WIN:(e // 2) * 2 * WIN + (jj + 1) * WIN],
                                           vab[r:r + QD, tile, 1 - jj, e * QD:(e + 1) * QD],
                                           pT[r:r + QD, tile % 2, (e % 2) * 2 + e // 2, jj * WIN:(jj + 1) * WIN],
                                           start=True, stop=True)
                mm.then_inc(pv_mm, 1)

            def output(l, w, tile):
                if tile == 0:
                    pe.wait_ge(wo_in, 16 * (l * PASSES + w + 1))
                pe.wait_ge(pv_out, units(l, w, tile))
                if isinstance(w, int) and w == PASSES - 1 and tile >= 2:
                    pe.wait_ge(att_done, units(l, w, tile) - 1)
                else:
                    pe.wait_ge(s_out, units(l, w, tile) + 2)
                for k in range(2):
                    mm = pe.matmul(PS[:, BS, BO:BO + P], wog[:, k, :], oT[:, k, tile * P:(tile + 1) * P],
                                   start=(k == 0), stop=(k == 1))
                mm.then_inc(wo_mm, 1)

            def step(l, it, s):
                tile2, w2_, live2 = stage(s, it, 2)
                tile3, w3, live3 = stage(s, it, 3)
                tile0, w0, live0 = stage(s, it, 0)
                tile4, w4, live4 = stage(s, it, LAST)
                if live2:
                    rotated_T(l, w2_, tile2)
                if live0:
                    project_qk(l, w0, tile0)
                if live2:
                    scores(l, w2_, tile2)
                if live3:
                    probs_T(l, w3, tile3)
                if live0:
                    project_v(l, w0, tile0)
                if live4:
                    output(l, w4, tile4)
                if live3:
                    times_v(l, w3, tile3)

            def before(l):
                pe.wait_ge(w_in, 32 * (l + 1))

            def ffn(l):
                def mean(b):
                    pe.wait_ge(ff_x[b], 32 * (l + 1))
                    if b >= 2:
                        pe.wait_ge(ff_c, l * B + b - 1)
                    pe.matmul(PS[:, 6 * (b % 2), :], onesm[:], fx[:, b, :], start=True, stop=True).then_inc(ff_mean, 1)

                def var(b):
                    pe.wait_ge(ff_sq, l * B + b + 1)
                    if b >= 2:
                        pe.wait_ge(ff_vr, l * B + b - 1)
                    pe.matmul(PS[:, 1 + b % 2, :], onesm[:], fsq[:, b, :], start=True, stop=True).then_inc(ff_var, 1)

                def gates(b):
                    pe.wait_ge(ff_h, l * B + b + 1)
                    for r in range(FK):
                        if b:
                            pe.wait_ge(ff_g, (l * B + b - 1) * FK + r + 1)
                        pe.matmul(PS[0:FR[r], 3 + r, :], w1[:, FF + r * P:FF + r * P + FR[r]], fh[:, b, :],
                                  start=True, stop=True).then_inc(ff_gm, 1)

                def values(b):
                    for r in range(FK):
                        if b:
                            pe.wait_ge(ff_a, (l * B + b - 1) * FK + r + 1)
                        pe.matmul(PS[0:FR[r], (6, 7, 0)[r], :], w1[:, r * P:r * P + FR[r]], fh[:, b, :],
                                  start=True, stop=True).then_inc(ff_am, 1)

                def second(b):
                    if b:
                        pe.wait_ge(ff_new, l * B + b)
                    for r in range(FK):
                        pe.wait_ge(ff_a, (l * B + b) * FK + r + 1)
                        mm = pe.matmul(PS[:, 1, :], w2[0:FR[r], r, :], fa[0:FR[r], r, :],
                                       start=(r == 0), stop=(r == FK - 1))
                    mm.then_inc(ff_ym, 1)

                pe.wait_ge(ffw_in, 48 * (l + 1))
                mean(0)
                mean(1)
                for b in range(B):
                    if b + 2 < B:
                        mean(b + 2)
                    var(b)
                gates(0)
                values(0)
                for b in range(1, B):
                    gates(b)
                    second(b - 1)
                    values(b)
                second(B - 1)

            pe.wait_ge(zeroed, 1)
            for credit in (v_mm, wo_mm):
                pe.sem_inc(credit)
            layers(pe, step, before, ffn)

        @block.scalar
        def _(act):
            def exps(l, w, tile):
                act.wait_ge(d_ready, units(l, w, tile))
                act.activation(pex[:, tile % 2], smd[:, tile % 2], ACT.Exp).then_inc(e_ready, 1)

            def log_norms(l, w, tile):
                act.wait_ge(sq_ready, units(l, w, tile))
                act.activation(lnss[:], ssq[:, tile % 2, :], ACT.Ln).then_inc(ln_ready, 1)

            def inverse_norms(l, w, tile):
                act.wait_ge(ln_ready, units(l, w, tile))
                act.activation(rn[:, tile % 2, :], lnss[:], ACT.Exp, scale=-0.5).then_inc(rn_ready, 1)

            def rotated_out(l, w, tile):
                act.wait_ge(rt_tr, units(l, w, tile))
                act.activation(qT[:, tile % 2], PS[:, BRT, 0:2 * P].rearrange("p (a n) -> p a n", a=2), ACT.Copy)
                act.activation(kT[:, :, WIN + tile * P:WIN + (tile + 1) * P],
                               PS[:, BRT, 2 * P:4 * P].rearrange("p (a n) -> p a n", a=2), ACT.Copy).then_inc(rt_out, 1)

            def qk_copy(l, w, tile):
                act.wait_ge(qk_mm, units(l, w, tile))
                if not first(w, tile):
                    act.wait_ge(sq_sum, units(l, w, tile) - 1)
                if not first(w, tile, 2):
                    act.wait_ge(n_ready, units(l, w, tile) - 2)
                act.activation(qk[:, tile % 2].rearrange("p a h d -> p (a h d)"), PS[:, BQK, :], ACT.Copy)
                act.activation(qksq[:].rearrange("p a h d -> p (a h d)"), PS[:, BQK, :], ACT.Square).then_inc(qk_out, 1)

            def probs_out(l, w, tile):
                act.wait_ge(pt_tr, units(l, w, tile))
                for half in range(2):
                    r = QD * half
                    act.activation(pT[r:r + QD, tile % 2],
                                   PS[r:r + QD, BPT, :].rearrange("p (k n) -> p k n", k=GH)
                                   [:, :, half * 2 * WIN:(half + 1) * 2 * WIN], ACT.Copy).then_inc(pt_out, 1)

            def v_copy(l, w, tile):
                act.wait_ge(v_mm, 1 + units(l, w, tile))
                if not first(w, tile, NT):
                    act.wait_ge(v_sh[tile], (16 if tile == NT - 1 else 32) * (l * PASSES + w))
                act.activation(vab[:, tile, 0, :], PS[:, BV, 0:GW], ACT.Copy).then_inc(v_out, 1)

            def o_copy(l, w, tile):
                act.wait_ge(pv_mm, units(l, w, tile))
                for half in range(2):
                    lo = tile * P + half * 2 * WIN
                    ins = act.activation(oT[:, :, lo:lo + 2 * WIN],
                                         PS[:, BPV[half], 0:4 * WIN].rearrange("p (a n) -> p a n", a=2), ACT.Copy)
                ins.then_inc(pv_out, 1)

            def step(l, it, s):
                tile2, w2_, live2 = stage(s, it, 2)
                tile3, w3, live3 = stage(s, it, 3)
                tile0, w0, live0 = stage(s, it, 0)
                if live2:
                    rotated_out(l, w2_, tile2)
                if live0:
                    qk_copy(l, w0, tile0)
                if live3:
                    probs_out(l, w3, tile3)
                if live0:
                    v_copy(l, w0, tile0)
                if live0:
                    log_norms(l, w0, tile0)
                if live2:
                    exps(l, w2_, tile2)
                if live0:
                    inverse_norms(l, w0, tile0)
                if live3:
                    o_copy(l, w3, tile3)

            def before(l):
                exp_ln_table(nc)

            def ffn(l):
                def square(b):
                    act.wait_ge(ff_c, l * B + b + 1)
                    act.activation(fsq[:, b, :], fc[:, b, :], ACT.Square).then_inc(ff_sq, 1)

                def rstd(b):
                    act.wait_ge(ff_var, l * B + b + 1)
                    act.activation(flv[:, b, :], PS[:, 1 + b % 2, :], ACT.Ln, bias=epsc[:, 0:1]).then_inc(ff_lv, 1)
                    act.wait_ge(ff_lv, l * B + b + 1)
                    act.activation(frs[:, b, :], flv[:, b, :], ACT.Exp, scale=-0.5).then_inc(ff_rs, 1)

                def scale(b):
                    act.wait_ge(ff_n, l * B + b + 1)
                    act.activation(fh[:, b, :], fn[:, b, :], ACT.Identity, scale=ffp[:, 2 * FK + 1:2 * FK + 2],
                                   bias=ffp[:, 2 * FK + 2:2 * FK + 3]).then_inc(ff_h, 1)

                act.wait_ge(ffw_in, 48 * (l + 1))
                square(0)
                square(1)
                for b in range(B + 2):
                    if b + 2 < B:
                        square(b + 2)
                    if b < B:
                        rstd(b)
                    if b >= 2:
                        scale(b - 2)
                for b in range(B):
                    for r in range(FK):
                        act.wait_ge(ff_gm, (l * B + b) * FK + r + 1)
                        if b:
                            act.wait_ge(ff_a, (l * B + b - 1) * FK + r + 1)
                        act.activation(fg[0:FR[r], r, :], PS[0:FR[r], 3 + r, :], ACT.Gelu,
                                       bias=ffp[0:FR[r], FK + r:FK + r + 1]).then_inc(ff_g, 1)

            layers(act, step, before, ffn)

        @block.gpsimd
        def _(pool):
            pool.memset(vab[0:WIN, 0, 1, :], 0.0)
            pool.memset(kT[:, :, 0:WIN], 0.0).then_inc(zeroed, 1)

            def rotate(l, w, tile):
                pool.wait_ge(n_ready, units(l, w, tile))
                for half in range(2):
                    a, c = half * HW, (1 - half) * HW
                    ins = pool.tensor_tensor(qks[:, tile % 2, :, :, a:a + HW], qkn[:, tile % 2, :, :, c:c + HW],
                                             rs[:, tile, :, a:a + HW].unsqueeze(2).to_broadcast([P, 2, GH, HW]),
                                             ALU.mult)
                ins.then_inc(sin_done, 1)
                pool.wait_ge(sin_done, units(l, w, tile))
                pool.wait_ge(cos_done, units(l, w, tile))
                pool.tensor_tensor(qkr[:, tile % 2], qkc[:, tile % 2], qks[:, tile % 2], ALU.add).then_inc(r_ready, 1)

            def probs_again(l, w, tile):
                pool.wait_ge(zi_ready, units(l, w, tile))
                pool.tensor_tensor(pn[:, tile % 2, :, 1, :], pex[:, tile % 2],
                                   zinv[:, tile % 2, :].unsqueeze(2).to_broadcast([P, GH, 2 * WIN]),
                                   ALU.mult).then_inc(p2_ready, 1)

            def step(l, it, s):
                tile3, w3, live3 = stage(s, it, 3)
                tile1, w1_, live1 = stage(s, it, 1)
                if live3:
                    probs_again(l, w3, tile3)
                if live1:
                    rotate(l, w1_, tile1)

            def before(l):
                pool.wait_ge(scaled, 1 + 2 * l + 2)

            def ffn(l):
                for b in range(B):
                    pool.wait_ge(ff_rs, l * B + b + 1)
                    pool.wait_ge(ff_c, l * B + b + 1)
                    pool.tensor_tensor(fu[:, b, :], fc[:, b, :], frs[:, b, :], ALU.mult).then_inc(ff_u, 1)

            layers(pool, step, before, ffn)

        @block.vector
        def _(v):
            def prob_sums(l, w, tile):
                v.wait_ge(e_ready, units(l, w, tile))
                v.tensor_reduce(zsum[:], pex[:, tile % 2], AX.X, ALU.add).then_inc(z_ready, 1)

            def inverse_sums(l, w, tile):
                v.wait_ge(z_ready, units(l, w, tile))
                v.reciprocal(zinv[:, tile % 2, :], zsum[:]).then_inc(zi_ready, 1)

            def normalise(l, w, tile):
                v.wait_ge(zi_ready, units(l, w, tile))
                v.tensor_tensor(pn[:, tile % 2, :, 0, :], pex[:, tile % 2],
                                zinv[:, tile % 2, :].unsqueeze(2).to_broadcast([P, GH, 2 * WIN]),
                                ALU.mult).then_inc(p_ready, 1)

            def unit_qk(l, w, tile):
                v.wait_ge(rn_ready, units(l, w, tile))
                if not first(w, tile, 2):
                    v.wait_ge(r_ready, units(l, w, tile) - 2)
                v.tensor_tensor(qkn[:, tile % 2].rearrange("p a h d -> p (a h) d"),
                                qk[:, tile % 2].rearrange("p a h d -> p (a h) d"),
                                rn[:, tile % 2, :].unsqueeze(2).to_broadcast([P, 2 * GH, QD]), ALU.mult).then_inc(n_ready, 1)

            def cosines(l, w, tile):
                v.wait_ge(n_ready, units(l, w, tile))
                v.tensor_tensor(qkc[:, tile % 2], qkn[:, tile % 2], rc[:, tile].unsqueeze(2).to_broadcast([P, 2, GH, QD]),
                                ALU.mult).then_inc(cos_done, 1)

            def square_sums(l, w, tile):
                v.wait_ge(qk_out, units(l, w, tile))
                v.tensor_reduce(ssr[:], qksq[:].rearrange("p a h d -> p (a h) d"), AX.X, ALU.add).then_inc(sq_sum, 1)

            def clamp(l, w, tile):
                v.wait_ge(sq_sum, units(l, w, tile))
                v.tensor_scalar(ssq[:, tile % 2, :], ssr[:], NORM_MIN * NORM_MIN, None, ALU.max).then_inc(sq_ready, 1)

            def masked_scores(l, w, tile):
                v.wait_ge(s_mm, units(l, w, tile))
                k = 0 if tile == 0 else 1
                v.scalar_tensor_tensor(sm[:].rearrange("p (a c) n -> p a (c n)", a=2), PS[:, BS:BS + 2, 0:4 * WIN],
                                       QK_SCALE, amask[:, k].rearrange("p (a n) -> p a n", a=2),
                                       ALU.mult, ALU.add).then_inc(s_out, 1)

            def maxima(l, w, tile):
                v.wait_ge(s_out, units(l, w, tile))
                v.tensor_reduce(smx[:], sm[:], AX.X, ALU.max).then_inc(mx_ready, 1)

            def less_maxima(l, w, tile):
                v.wait_ge(mx_ready, units(l, w, tile))
                v.tensor_tensor(smd[:, tile % 2], sm[:], smx[:].unsqueeze(2).to_broadcast([P, GH, 2 * WIN]),
                                ALU.subtract).then_inc(d_ready, 1)

            def add_output(l, w, tile):
                v.wait_ge(wo_mm, 1 + units(l, w, tile))
                xa = XA[:, w % B, 1 + tile * P:1 + (tile + 1) * P]
                v.tensor_tensor(xa, PS[:, BS, BO:BO + P], xa, ALU.add).then_inc(att_done, 1)

            def step(l, it, s):
                tile1, w1_, live1 = stage(s, it, 1)
                tile2, w2_, live2 = stage(s, it, 2)
                tile3, w3, live3 = stage(s, it, 3)
                tile0, w0, live0 = stage(s, it, 0)
                tile4, w4, live4 = stage(s, it, LAST)
                if live3:
                    prob_sums(l, w3, tile3)
                if live1:
                    unit_qk(l, w1_, tile1)
                if live3:
                    inverse_sums(l, w3, tile3)
                if live1:
                    cosines(l, w1_, tile1)
                if live3:
                    normalise(l, w3, tile3)
                if live2:
                    masked_scores(l, w2_, tile2)
                if live0:
                    square_sums(l, w0, tile0)
                if live2:
                    maxima(l, w2_, tile2)
                if live0:
                    clamp(l, w0, tile0)
                if live2:
                    less_maxima(l, w2_, tile2)
                if live4:
                    add_output(l, w4, tile4)

            def before(l):
                v.wait_ge(w_in, 32 * (l + 1))
                for dst, src, k in ((rc, rotc, 0), (rs, rots, 1)):
                    v.tensor_tensor(dst[:], src[:], qkg[:, k].unsqueeze(1).to_broadcast([P, NT, 2, QD]),
                                    ALU.mult).then_inc(scaled, 1)
                v.wait_ge(scaled, 1 + 2 * l + 2)

            def ffn(l):
                def centre(b):
                    v.wait_ge(ff_mean, l * B + b + 1)
                    v.tensor_tensor(fc[:, b, :], fx[:, b, :], PS[:, 6 * (b % 2), :], ALU.subtract).then_inc(ff_c, 1)

                def scale(b):
                    v.wait_ge(ff_rs, l * B + b + 1)
                    r = frs[:, b, :]
                    v.scalar_tensor_tensor(fvr[:, b, :], PS[:, 1 + b % 2, :], epsc[:, 0:1], r, ALU.add, ALU.mult).then_inc(ff_vr, 1)
                    v.wait_ge(ff_vr, l * B + b + 1)
                    v.scalar_tensor_tensor(fvrr[:, b, :], fvr[:, b, :], -0.5, r, ALU.mult, ALU.mult).then_inc(ff_vrr, 1)
                    v.wait_ge(ff_vrr, l * B + b + 1)
                    v.wait_ge(ff_u, l * B + b + 1)
                    v.scalar_tensor_tensor(fn[:, b, :], fvrr[:, b, :], 1.5, fu[:, b, :], ALU.add, ALU.mult).then_inc(ff_n, 1)

                def new_state(b):
                    v.wait_ge(ff_ym, l * B + b + 1)
                    v.scalar_tensor_tensor(X[:, b, PADX:PADX + L], PS[:, 1, :], ffp[:, 2 * FK:2 * FK + 1],
                                           XA[:, b, 1:1 + L], ALU.add, ALU.add).then_inc(ff_new, 1)
                    v.wait_ge(ff_new, l * B + b + 1)
                    v.tensor_copy(XA[:, b, 1:1 + L], X[:, b, PADX:PADX + L]).then_inc(ff_done, 1)

                v.wait_ge(att_done, UNITS * (l + 1))
                v.wait_ge(ffw_in, 48 * (l + 1))
                for b in range(B):
                    centre(b)
                for b in range(B):
                    scale(b)
                for b in range(B):
                    for r in range(FK):
                        v.wait_ge(ff_am, (l * B + b) * FK + r + 1)
                        v.wait_ge(ff_g, (l * B + b) * FK + r + 1)
                        if b:
                            v.wait_ge(ff_ym, l * B + b)
                        v.scalar_tensor_tensor(fa[0:FR[r], r, :], PS[0:FR[r], (6, 7, 0)[r], :], ffp[0:FR[r], r:r + 1],
                                               fg[0:FR[r], r, :], ALU.add, ALU.mult).then_inc(ff_a, 1)
                    if b:
                        new_state(b - 1)
                new_state(B - 1)
                v.wait_ge(ff_done, B * (l + 2))

            v.wait_ge(tables, 48)
            for credit in (scaled,) + (ff_done,) * B:
                v.sem_inc(credit)
            layers(v, step, before, ffn)


def attention_and_experts(nc, t, XR, X, mod, PS, onesm, ident, epsc, sel8, out):
    with ExitStack() as ctx:
        def sb(name, shape):
            return ctx.enter_context(nc.sbuf_tensor(name, shape, F32))

        def sem(name):
            return ctx.enter_context(nc.semaphore(name))

        PAIR = AH // 2
        NP = NT * PAIR
        aq = sb("aq", [P, AH * AD])
        akd = sb("akd", [P, AR])
        akv = sb("akv", [AR, 2, AH * AD])
        awo = sb("awo", [P, 2, D])
        rw = sb("rw", [P, NE])
        rb = sb("rb", [P, NE])
        ridx = sb("ridx", [P, NE])
        sw13 = sb("sw13", [P, 2, 2 * P])
        sw2 = sb("sw2", [P, 2, D])
        ew1 = sb("ew1", [P, NE, P])
        ew2 = sb("ew2", [P, NE, D])
        lnc = sb("c_lnc", [P, L])
        lnsq = sb("c_lnsq", [P, L])
        lnv = sb("c_lnv", [P, L])
        lnr = sb("c_lnr", [P, L])
        lnt = sb("c_lnt", [P, L])
        h1T = sb("c_h1T", [P, L])
        hT = sb("c_hT", [P, L])
        qz = sb("qz", [P, AH, L])
        kT = sb("c_kT", [P, 2, L])
        lat = sb("c_lat", [AR, L])
        vt = sb("c_v", [P, NT, AH * AD])
        amx = sb("amx", [P, 2, 2])
        anm = sb("anm", [P, 2, 2])
        prob = sb("prob", [P, 4, L])
        probT = sb("probT", [P, 4, NT, P])
        asum = sb("asum", [P, NT, AH])
        arz = sb("arz", [P, NT, AH])
        aoT = sb("aoT", [P, 2, L])
        rsg = sb("rsg", [P, NT, NE])
        rt = sb("rt", [P, 10, NT, NE])
        rm = sb("rm", [P, 12, NT])
        comb = sb("comb", [P, NT, NE])
        combT = sb("combT", [P, L])
        shs = sb("shs", [P, 2, L])
        shg = sb("shg", [P, 2, L])
        eh = sb("eh", [P, 2, L])
        eg = sb("eg", [P, 2, L])
        res = sb("res", [P, L])

        weights = sem("c_weights")
        zeroed = sem("c_zeroed")
        dve_steps = sem("c_dve_steps")
        ln_in = sem("c_ln_in")
        ln_mean = sem("c_ln_mean")
        ln_cent = sem("c_ln_cent")
        ln_sq = sem("c_ln_sq")
        ln_var = sem("c_ln_var")
        ln_lv = sem("c_ln_lv")
        ln_rstd = sem("c_ln_rstd")
        h_ready = sem("c_h_ready")
        prj_mm = sem("prj_mm")
        q_mm = sem("q_mm")
        prj_out = sem("prj_out")
        q_out = [sem("q_out_dve"), sem("q_out_act")]
        sc_mm = sem("sc_mm")
        max_in = sem("max_in")
        max_ready = sem("max_ready")
        prob_ready = sem("prob_ready")
        pt_tr = sem("c_pt_tr")
        pt_out = [sem("pt_out_dve"), sem("pt_out_act")]
        o_mm = sem("o_mm")
        rz_ready = sem("rz_ready")
        pn_ready = sem("c_pn_ready")
        ot_out = sem("ot_out")
        ay_mm = sem("ay_mm")
        rt_mm = sem("rt_mm")
        sig_ready = sem("sig_ready")
        comb_ready = sem("comb_ready")
        ct_tr = sem("ct_tr")
        ct_out = sem("ct_out")
        sh_mm = sem("sh_mm")
        sh_silu = sem("sh_silu")
        sh_ready = sem("sh_ready")
        eh_mm = sem("eh_mm")
        cb_mm = sem("cb_mm")
        eh_ready = sem("eh_ready")
        eg_ready = sem("eg_ready")
        ey_mm = sem("ey_mm")
        res_ready = sem("res_ready")
        stored = sem("stored")

        WEIGHTS = [(aq, "aq"), (akd, "akd"), (akv, "akv"), (awo, "awo"), (rw, "rw"), (rb, "rb"), (ridx, "ridx"),
                   (sw13, "sw13"), (sw2, "sw2"), (ew1, "ew1"), (ew2, "ew2")]
        NPRJ = 4
        block = ctx.enter_context(nc.Block())

        @block.sync
        def _(sp):
            for dst, name in WEIGHTS:
                sp.dma_start(dst[:], t[name]).then_inc(weights, 16)
            sp.sem_inc(stored, 16)
            with sp.Fori(0, B) as b:
                sp.wait_ge(res_ready, b + 2)
                sp.dma_start(out[:, b, :], res[:]).then_inc(stored, 16)
            sp.wait_ge(weights, 16 * len(WEIGHTS))
            sp.wait_ge(stored, 16 * (B + 1))

        @block.tensor
        def _(pe):
            pe.wait_ge(weights, 16 * len(WEIGHTS))

            def mean(b, k):
                pe.matmul(PS[:, 0 if k else 2, :], onesm[:], XR[:, b % B, :], start=True, stop=True).then_inc(ln_mean, 1)

            def var(b, k):
                pe.wait_ge(ln_sq, 2 * b + k + 1)
                pe.matmul(PS[:, 1, :], onesm[:], lnsq[:], start=True, stop=True).then_inc(ln_var, 1)

            pe.wait_ge(ln_in, 1)
            mean(0, 0)
            var(0, 0)
            with pe.Fori(0, B) as b:
                pe.wait_ge(h_ready, 2 * b + 1)
                pe.matmul(PS[0:AR, 4, :], akd[:], h1T[:], start=True, stop=True).then_inc(prj_mm, 1)
                for m in range(2):
                    pe.matmul(PS[:, 2 + m, :], aq[:, m * P:(m + 1) * P], h1T[:], start=True, stop=True).then_inc(q_mm, 1)
                pe.wait_ge(prj_out, NPRJ * b + 1)
                for m in range(2):
                    pe.matmul(PS[:, 5 + m, :], akv[:, 0, m * P:(m + 1) * P], lat[:], start=True, stop=True).then_inc(prj_mm, 1)
                pe.wait_ge(res_ready, b + 1)
                for i in range(NT):
                    mm = pe.matmul(PS[:, i // 2, (i % 2) * AH * AD:(i % 2 + 1) * AH * AD], lat[:, i * P:(i + 1) * P],
                                   akv[:, 1, :], start=True, stop=True)
                mm.then_inc(prj_mm, 1)
                pe.wait_ge(prj_out, NPRJ * b + NPRJ)
                for done in q_out:
                    pe.wait_ge(done, AH // 2 * (b + 1))

                def score(p):
                    if p >= 2:
                        pe.wait_ge(prob_ready, 2 * NP * b + 2 * (p - 1))
                    i, hp = p // PAIR, p % PAIR
                    for q in range(2):
                        h = 2 * hp + q
                        mm = pe.matmul(PS[:, 2 * (p % 2) + q, :], qz[:, h, i * P:(i + 1) * P], kT[:, h // 4, :],
                                       start=True, stop=True)
                    mm.then_inc(sc_mm, 1)

                def prob_T(p):
                    pe.wait_ge(pn_ready, NP * b + p + 1)
                    for q in range(2):
                        u = 2 * p + q
                        if p:
                            pe.wait_ge(pt_out[q], NP * b + p)
                        for k in range(NT):
                            mm = pe.transpose(PS[:, 4 + q, k * P:(k + 1) * P], prob[:, u % 4, k * P:(k + 1) * P],
                                              ident[:])
                        mm.then_inc(pt_tr, 1)

                def times_v(p):
                    i, hp = p // PAIR, p % PAIR
                    for q in range(2):
                        pe.wait_ge(pt_out[q], NP * b + p + 1)
                    for k in range(NT):
                        for q in range(2):
                            h = 2 * hp + q
                            r = AD * (h % 4)
                            mm = pe.matmul(PS[r:r + AD, 6 + h // 4, i * P:(i + 1) * P], vt[:, k, h * AD:(h + 1) * AD],
                                           probT[:, (2 * p + q) % 4, k, :], start=(k == 0), stop=(k == NT - 1),
                                           tile_position=(0, r))
                    mm.then_inc(o_mm, 1)

                score(0)
                for p in range(NP + 2):
                    if p + 1 < NP:
                        score(p + 1)
                    if p >= 2:
                        times_v(p - 2)
                    if 1 <= p <= NP:
                        prob_T(p - 1)
                for m in range(2):
                    pe.wait_ge(ot_out, 2 * b + m + 1)
                    mm = pe.matmul(PS[:, 0, :], awo[:, m, :], aoT[:, m, :], start=(m == 0), stop=(m == 1))
                mm.then_inc(ay_mm, 1)

                pe.wait_ge(ln_in, b + 2)
                mean(b, 1)
                var(b, 1)
                pe.wait_ge(h_ready, 2 * b + 2)
                for i in range(NT):
                    mm = pe.matmul(PS[:, 2, i * NE:(i + 1) * NE], hT[:, i * P:(i + 1) * P], rw[:], start=True, stop=True)
                mm.then_inc(rt_mm, 1)
                for k in range(2):
                    for m in range(2):
                        pe.matmul(PS[:, 4 + 2 * k + m, :], sw13[:, k, m * P:(m + 1) * P], hT[:],
                                  start=True, stop=True).then_inc(sh_mm, 1)
                pe.wait_ge(sh_ready, 2 * b + 2)
                for m in range(2):
                    pe.matmul(PS[:, 0, :], sw2[:, m, :], shg[:, m, :], start=(m == 0), stop=False)
                pe.wait_ge(comb_ready, b + 1)
                for i in range(NT):
                    mm = pe.transpose(PS[0:NE, 3, i * P:(i + 1) * P], comb[:, i, :], ident[:])
                mm.then_inc(ct_tr, 1)
                pe.wait_ge(ct_out, b + 1)

                def hidden(e):
                    if e >= 2:
                        pe.wait_ge(eh_ready, NE * b + e - 1)
                    pe.matmul(PS[:, 4 + e % 2, :], ew1[:, e, :], hT[:], start=True, stop=True).then_inc(eh_mm, 1)
                    if e >= 2:
                        pe.wait_ge(eg_ready, NE * b + e - 1)
                    pe.matmul(PS[:, 6 + e % 2, :], sel8[:, e, :], combT[:], start=True, stop=True).then_inc(cb_mm, 1)

                hidden(0)
                for e in range(NE):
                    if e + 1 < NE:
                        hidden(e + 1)
                    if e == 0:
                        mean(b + 1, 0)
                    if e == 3:
                        var(b + 1, 0)
                    pe.wait_ge(eg_ready, NE * b + e + 1)
                    pe.matmul(PS[:, 0, :], ew2[:, e, :], eg[:, e % 2, :], start=False, stop=(e == NE - 1)).then_inc(ey_mm, 1)

        @block.scalar
        def _(act):
            act.wait_ge(weights, 16 * len(WEIGHTS))
            act.wait_ge(zeroed, 1)

            def square(b, k):
                act.wait_ge(ln_cent, 2 * b + k + 1)
                act.activation(lnsq[:], lnc[:], ACT.Square).then_inc(ln_sq, 1)

            def rstd(b, k):
                act.wait_ge(ln_var, 2 * b + k + 1)
                act.activation(lnv[:], PS[:, 1, :], ACT.Ln, bias=epsc[:, 0:1]).then_inc(ln_lv, 1)
                act.wait_ge(ln_lv, 2 * b + k + 1)
                act.activation(lnr[:], lnv[:], ACT.Exp, scale=-0.5).then_inc(ln_rstd, 1)

            exp_ln_table(nc)
            square(0, 0)
            rstd(0, 0)
            with act.Fori(0, B) as b:
                exp_ln_table(nc)
                prj = [(lat[:], PS[0:AR, 4, :]), (kT[:, 0, :], PS[:, 5, :]), (kT[:, 1, :], PS[:, 6, :]),
                       (vt[:].rearrange("p i n -> p (i n)"), PS[:, 0:2, :].rearrange("p a n -> p (a n)"))]
                for n, (dst, src) in enumerate(prj):
                    act.wait_ge(prj_mm, NPRJ * b + n + 1)
                    act.activation(dst, src, ACT.Copy).then_inc(prj_out, 1)
                    if n == 0:
                        for h in range(AH // 2, AH):
                            r = AD * (h % 4)
                            if h == AH // 2:
                                act.wait_ge(q_mm, 2 * b + 2)
                            act.activation(qz[r:r + AD, h, :], PS[r:r + AD, 3, :], ACT.Copy).then_inc(q_out[1], 1)

                for p in range(NP + 1):
                    if p < NP:
                        i, hp = p // PAIR, p % PAIR
                        act.wait_ge(max_ready, NP * b + p + 1)
                        for q in range(2):
                            u, h = 2 * p + q, 2 * hp + q
                            if p >= 2:
                                act.wait_ge(pt_tr, 2 * NP * b + u - 3)
                            act.activation(prob[:, u % 4, :], PS[:, 2 * (p % 2) + q, :], ACT.Exp,
                                           bias=anm[:, p % 2, q:q + 1], scale=SM_SCALE,
                                           accum_out=asum[:, i, h:h + 1]).then_inc(prob_ready, 1)
                    if p:
                        act.wait_ge(pt_tr, 2 * NP * b + 2 * p)
                        act.activation(probT[:, (2 * p - 1) % 4].rearrange("p a n -> p (a n)"), PS[:, 5, :],
                                       ACT.Copy).then_inc(pt_out[1], 1)
                square(b, 1)
                rstd(b, 1)
                act.wait_ge(rt_mm, b + 1)
                act.activation(rsg[:].rearrange("p i e -> p (i e)"), PS[:, 2, 0:NT * NE], ACT.Sigmoid).then_inc(sig_ready, 1)
                for m in range(2):
                    act.wait_ge(sh_mm, 4 * b + m + 1)
                    act.activation(shs[:, m, :], PS[:, 4 + m, :], ACT.Silu).then_inc(sh_silu, 1)
                for e in range(NE):
                    act.wait_ge(eh_mm, NE * b + e + 1)
                    if e >= 2:
                        act.wait_ge(eg_ready, NE * b + e - 1)
                    act.activation(eh[:, e % 2, :], PS[:, 4 + e % 2, :], ACT.Gelu).then_inc(eh_ready, 1)
                    if e == 1:
                        square(b + 1, 0)
                    if e == 4:
                        exp_ln_table(nc)
                        rstd(b + 1, 0)

        @block.gpsimd
        def _(pool):
            pool.memset(combT[:], 0.0)
            pool.memset(qz[:], 0.0).then_inc(zeroed, 1)
            pool.wait_ge(weights, 16 * len(WEIGHTS))

        @block.vector
        def _(v):
            st = Steps(v, dve_steps)
            v.wait_ge(weights, 16 * len(WEIGHTS))
            v.wait_ge(zeroed, 1)

            def link(ins):
                st.did(ins)
                st.wait()

            def centre(b, k):
                v.wait_ge(ln_mean, b * 2 + k + 1)
                v.tensor_tensor(lnc[:], XR[:, b % B, :], PS[:, 0 if k else 2, :], ALU.subtract).then_inc(ln_cent, 1)

            def normed(b, k, dst, scale, shift):
                v.wait_ge(ln_rstd, b * 2 + k + 1)
                v.wait_ge(ln_cent, b * 2 + k + 1)
                link(v.scalar_tensor_tensor(lnv[:], PS[:, 1, :], epsc[:, 0:1], lnr[:], ALU.add, ALU.mult))
                link(v.scalar_tensor_tensor(lnt[:], lnv[:], -0.5, lnr[:], ALU.mult, ALU.mult))
                link(v.scalar_tensor_tensor(lnv[:], lnt[:], 1.5, lnr[:], ALU.add, ALU.mult))
                link(v.tensor_tensor(lnt[:], lnc[:], lnv[:], ALU.mult))
                v.tensor_scalar(dst, lnt[:], scale, shift, ALU.mult, ALU.add).then_inc(h_ready, 1)

            def attention_input(b):
                normed(b, 0, h1T[:], mod[:, 1, 1, bass.ds(b % B, 1)], mod[:, 1, 0, bass.ds(b % B, 1)])

            for k in range(B):
                ins = v.scalar_tensor_tensor(XR[:, k, :], X[:, k, PADX:PADX + L], mod[:, 0, 5, k:k + 1], XR[:, k, :],
                                             ALU.mult, ALU.add)
            ins.then_inc(ln_in, 1)
            v.wait_ge(ln_in, 1)
            v.sem_inc(res_ready)
            centre(0, 0)
            attention_input(0)
            PER = 30
            with v.Fori(0, B) as b:
                st.enter(b, PER)
                for h in range(AH // 2):
                    r = AD * (h % 4)
                    if h == 0:
                        v.wait_ge(q_mm, 2 * b + 1)
                    v.tensor_copy(qz[r:r + AD, h, :], PS[r:r + AD, 2, :]).then_inc(q_out[0], 1)

                def row_max(p):
                    v.wait_ge(sc_mm, NP * b + p + 1)
                    v.tensor_reduce(amx[:, p % 2, :], PS[:, 2 * (p % 2):2 * (p % 2) + 2, :], AX.X, ALU.max).then_inc(max_in, 1)
                    v.wait_ge(max_in, NP * b + p + 1)
                    if p >= 2:
                        v.wait_ge(prob_ready, 2 * NP * b + 2 * (p - 1))
                    v.tensor_scalar(anm[:, p % 2, :], amx[:, p % 2, :], -SM_SCALE, None, ALU.mult).then_inc(max_ready, 1)

                def normalise(p):
                    i, hp = p // PAIR, p % PAIR
                    v.wait_ge(prob_ready, 2 * NP * b + 2 * p + 2)
                    v.reciprocal(arz[:, i, 2 * hp:2 * hp + 2], asum[:, i, 2 * hp:2 * hp + 2]).then_inc(rz_ready, 1)
                    v.wait_ge(rz_ready, NP * b + p + 1)
                    for q in range(2):
                        slot = prob[:, (2 * p + q) % 4, :]
                        ins = v.tensor_scalar(slot, slot, arz[:, i, 2 * hp + q:2 * hp + q + 1], None, ALU.mult)
                    ins.then_inc(pn_ready, 1)

                row_max(0)
                for p in range(NP + 1):
                    if p + 1 < NP:
                        row_max(p + 1)
                    if p < NP:
                        normalise(p)
                    if p:
                        v.wait_ge(pt_tr, 2 * NP * b + 2 * p - 1)
                        v.tensor_copy(probT[:, (2 * p - 2) % 4].rearrange("p a n -> p (a n)"), PS[:, 4, :]).then_inc(pt_out[0], 1)
                v.wait_ge(o_mm, NP * b + NP)
                for m in range(2):
                    v.tensor_copy(aoT[:, m, :], PS[:, 6 + m, :]).then_inc(ot_out, 1)
                v.wait_ge(ay_mm, b + 1)
                v.scalar_tensor_tensor(XR[:, b, :], PS[:, 0, :], mod[:, 1, 2, bass.ds(b, 1)], XR[:, b, :],
                                       ALU.mult, ALU.add).then_inc(ln_in, 1)
                v.wait_ge(ln_in, b + 2)
                centre(b, 1)
                normed(b, 1, hT[:], mod[:, 1, 4, bass.ds(b, 1)], mod[:, 1, 3, bass.ds(b, 1)])

                v.wait_ge(sig_ready, b + 1)
                wide = lambda x: x.unsqueeze(2).to_broadcast([P, NT, NE])
                every = lambda x: x.unsqueeze(1).to_broadcast([P, NT, NE])
                link(v.tensor_tensor(rt[:, 0], rsg[:], every(rb[:]), ALU.add))
                for k in range(2):
                    sel, eq, idx, hot = rt[:, 4 * k], rt[:, 4 * k + 1], rt[:, 4 * k + 2], rt[:, 4 * k + 3]
                    link(v.tensor_reduce(rm[:, 2 * k, :], sel, AX.X, ALU.max))
                    link(v.tensor_tensor(eq, sel, wide(rm[:, 2 * k, :]), ALU.is_equal))
                    link(v.tensor_tensor(idx, eq, every(ridx[:]), ALU.mult))
                    link(v.tensor_reduce(rm[:, 2 * k + 1, :], idx, AX.X, ALU.max))
                    link(v.tensor_tensor(hot, idx, wide(rm[:, 2 * k + 1, :]), ALU.is_equal))
                    if k == 0:
                        link(v.scalar_tensor_tensor(rt[:, 4], hot, MASKED, sel, ALU.mult, ALU.add))
                link(v.tensor_tensor(rt[:, 8], rt[:, 3], rt[:, 7], ALU.add))
                link(v.tensor_tensor(rt[:, 9], rt[:, 8], rsg[:], ALU.mult))
                link(v.tensor_reduce(rm[:, 4, :], rt[:, 9], AX.X, ALU.add))
                link(v.tensor_scalar(rm[:, 5, :], rm[:, 4, :], DENOM_MIN, None, ALU.add))
                link(v.reciprocal(rm[:, 6, :], rm[:, 5, :]))
                link(v.tensor_scalar(rm[:, 7, :], rm[:, 4, :], DENOM_MIN, None, ALU.is_gt))
                link(v.tensor_tensor(rm[:, 8, :], rm[:, 6, :], rm[:, 7, :], ALU.mult))
                link(v.tensor_scalar(rm[:, 9, :], rm[:, 7, :], -0.5, 0.5, ALU.mult, ALU.add))
                link(v.tensor_tensor(rt[:, 1], rt[:, 9], wide(rm[:, 8, :]), ALU.mult))
                link(v.tensor_tensor(rt[:, 2], rt[:, 8], wide(rm[:, 9, :]), ALU.mult))
                v.tensor_tensor(comb[:], rt[:, 1], rt[:, 2], ALU.add).then_inc(comb_ready, 1)
                for m in range(2):
                    v.wait_ge(sh_silu, 2 * b + m + 1)
                    v.wait_ge(sh_mm, 4 * b + m + 3)
                    v.tensor_tensor(shg[:, m, :], shs[:, m, :], PS[:, 6 + m, :], ALU.mult).then_inc(sh_ready, 1)
                v.wait_ge(ct_tr, b + 1)
                v.tensor_copy(combT[0:NE, :], PS[0:NE, 3, :]).then_inc(ct_out, 1)
                for e in range(NE):
                    v.wait_ge(eh_ready, NE * b + e + 1)
                    v.wait_ge(cb_mm, NE * b + e + 1)
                    if e >= 2:
                        v.wait_ge(ey_mm, NE * b + e - 1)
                    v.tensor_tensor(eg[:, e % 2, :], eh[:, e % 2, :], PS[:, 6 + e % 2, :], ALU.mult).then_inc(eg_ready, 1)
                    if e == 0:
                        centre(b + 1, 0)
                    if e == 5:
                        attention_input(b + 1)
                v.wait_ge(ey_mm, NE * b + NE)
                v.wait_ge(stored, 16 * (b + 1))
                v.scalar_tensor_tensor(res[:], PS[:, 0, :], mod[:, 1, 5, bass.ds(b, 1)], XR[:, b, :],
                                       ALU.mult, ALU.add).then_inc(res_ready, 1)
                st.leave(B, PER)
            v.wait_ge(res_ready, B + 1)


def build(nc, t, out):
    with ExitStack() as ctx:
        def sb(name, shape):
            return ctx.enter_context(nc.sbuf_tensor(name, shape, F32))

        PS = ctx.enter_context(nc.psum_tensor("PS", [P, 8, 512], F32))
        XR = sb("XR", [P, B, L])
        X = sb("X", [P, B, PADX + L])
        XA = sb("XA", [P, B, 1 + L])
        mod = sb("mod", [P, 2, 6, B])
        onesm = sb("onesm", [P, P])
        ident = sb("ident", [P, P])
        epsc = sb("epsc", [P, 2])
        sel8 = sb("sel8", [P, 8, P])
        mixer(nc, t, XR, X, XA, mod, PS, onesm, ident, epsc, sel8)
        local_layers(nc, t, X, XA, PS, onesm, ident, epsc)
        attention_and_experts(nc, t, XR, X, mod, PS, onesm, ident, epsc, sel8, out)


def rows(w, k=P):
    return w.reshape(-1, k, w.shape[-1]).transpose(1, 0, 2)


def layout(a):
    f = np.float32
    h = {}
    h["xT"] = a["L0_attn_input_tensor"].reshape(B * L, D).T.reshape(D, B, L)
    h["cT"] = np.stack([a["L0_c"].T, a["L1_c"].T], 1)
    h["wmod"] = np.stack([a["L0_wmod"], a["L1_wmod"]], 1)
    h["wxz"] = np.stack([a["L0_attn_Wx"].T, a["L0_attn_Wz"].T], 1)
    conv = np.concatenate([a["L0_attn_conv_w"][:, 0, :], a["L0_attn_conv_b"][:, None]], 1)
    h["convp"] = rows(conv)
    h["wbc"] = np.stack([rows(a["L0_attn_Wb"].T), rows(a["L0_attn_Wc"].T)], 1)
    h["wdt"] = rows(a["L0_attn_Wdt"].T)
    h["head8"] = np.stack([a["L0_attn_b_dt"], a["L0_attn_log_a"]], 1)
    h["featp"] = rows(np.stack([np.repeat(a["L0_attn_d_param"], SP), a["L0_attn_gn_w"], a["L0_attn_gn_b"]], 1))
    h["wout"] = rows(a["L0_attn_Wout"].T)
    wqkv = a["L0_ffn_Wqkv"].reshape(DEPTH, D, 3, NG, GW).transpose(0, 1, 3, 2, 4)
    h["wqkv"] = wqkv.reshape(DEPTH, D, NG, 3 * GW)
    qk = np.stack([a["L0_ffn_q_scale"], a["L0_ffn_k_scale"]], 1)
    swapped = np.concatenate([qk[..., QD // 2:], qk[..., :QD // 2]], -1)
    h["qkg"] = np.broadcast_to(np.stack([qk, swapped], 1)[:, None], (DEPTH, P, 2, 2, QD))
    h["wo"] = a["L0_ffn_Wo"].reshape(DEPTH, NG, 2, P, D).transpose(0, 1, 3, 2, 4)
    h["w1"] = a["L0_ffn_W1"]
    w2 = np.zeros((DEPTH, FK * P, D), f)
    w2[:, :FF] = a["L0_ffn_W2"]
    h["w2"] = w2.reshape(DEPTH, FK, P, D).transpose(0, 2, 1, 3)
    ffp = np.zeros((DEPTH, P, 2 * FK + 3), f)
    for k in range(2):
        b1 = np.zeros((DEPTH, FK * P), f)
        b1[:, :FF] = a["L0_ffn_b1"][:, k * FF:(k + 1) * FF]
        ffp[:, :, k * FK:(k + 1) * FK] = b1.reshape(DEPTH, FK, P).transpose(0, 2, 1)
    ffp[:, :, 2 * FK] = a["L0_ffn_b2"]
    ffp[:, :, 2 * FK + 1] = a["L0_ffn_ln_g"]
    ffp[:, :, 2 * FK + 2] = a["L0_ffn_ln_b"]
    h["ffp"] = ffp
    h["aq"] = a["L1_attn_Wq"].T
    h["akd"] = a["L1_attn_Wkv_down"].T
    h["akv"] = np.stack([a["L1_attn_Wk_up"].T, a["L1_attn_Wv_up"].T], 1)
    h["awo"] = rows(a["L1_attn_Wo"].T)
    h["rw"] = a["L1_ffn_router_w"].T
    h["rb"] = np.broadcast_to(a["L1_ffn_router_bias"], (P, NE))
    h["sw13"] = np.stack([a["L1_ffn_sw1"], a["L1_ffn_sw3"]], 1)
    h["sw2"] = rows(a["L1_ffn_sw2"])
    h["ew1"] = a["L1_ffn_ew1"].transpose(1, 0, 2)
    h["ew2"] = a["L1_ffn_ew2"].transpose(1, 0, 2)
    h["onesm"] = np.full((P, P), 1.0 / D, f)
    h["ident"] = np.eye(P, dtype=f)
    h["sel8"] = np.repeat(np.eye(P, 8, dtype=f)[:, :, None], P, 2)
    h["tri"] = np.triu(np.ones((P, P), f))
    h["grpm"] = np.kron(np.eye(P // SP), np.full((SP, SP), 1.0 / SP)).astype(f)
    h["ridx"] = np.broadcast_to(np.arange(NE, 0, -1).astype(f), (P, NE))
    i = np.arange(P)[:, None] % WIN
    j = np.arange(2 * WIN)[None, :] - WIN
    off = (i < j) | (i > j + WIN)
    first = off | ((j < 0) & (np.arange(P)[:, None] < WIN))
    h["amask"] = np.tile(np.where(np.stack([first, off], 1), f(MASKED), f(0)), (1, 1, GH))
    half = np.arange(0, QD, 2, dtype=f)
    inv = f(1) / np.power(f(10000), half / f(QD), dtype=f)
    fr = (np.arange(L, dtype=f)[:, None] * inv[None]).astype(f).astype(np.float64)
    base = ((half + f(0.4 * QD)) / f(1.4 * QD)).astype(np.float64)
    power = (np.arange(L) - L // 2) / (WIN // 2)
    scale = base[None, :] ** power[:, None]
    two = lambda x, y: np.concatenate([x, y], -1)
    rotc = np.stack([two(np.cos(fr) * scale, np.cos(fr) * scale), two(np.cos(fr) / scale, np.cos(fr) / scale)], 1)
    rots = np.stack([two(-np.sin(fr) * scale, np.sin(fr) * scale), two(-np.sin(fr) / scale, np.sin(fr) / scale)], 1)
    h["rotc"] = rotc.reshape(NT, P, 2, QD).transpose(1, 0, 2, 3)
    h["rots"] = rots.reshape(NT, P, 2, QD).transpose(1, 0, 2, 3)
    return {"in_" + k: np.ascontiguousarray(v, dtype=f) for k, v in h.items()}


def kernel(**inputs):
    import concourse.bacc as bacc
    from concourse.bass_utils import run_bass_kernel_spmd

    nc = bacc.Bacc("TRN2", target_bir_lowering=False, num_devices=1)
    arrays = layout({k: np.asarray(v) for k, v in inputs.items()})
    t = {k[3:]: nc.dram_tensor(k, v.shape, F32, kind="ExternalInput").ap() for k, v in arrays.items()}
    out = nc.dram_tensor("out", (D, B, L), F32, kind="ExternalOutput").ap()
    build(nc, t, out)
    r = run_bass_kernel_spmd(nc, [arrays], core_ids=[0])
    return np.ascontiguousarray(r.results[0]["out"].reshape(D, B * L).T.reshape(B, L, D))
```
